# Optimizing a Trainium2 kernel written in Bass

```python
import numpy as np
import jax
import jax.numpy as jnp

def _softmax(x, axis=-1):
    return jax.nn.softmax(x, axis=axis)

def _gelu(x):
    return jax.nn.gelu(x, approximate=True)

def _silu(x):
    return jax.nn.silu(x)

def _sigmoid(x):
    return jax.nn.sigmoid(x)

def _layernorm(x, axis=-1, eps=1e-05):
    m = jnp.mean(x, axis=axis, keepdims=True)
    v = jnp.var(x, axis=axis, keepdims=True)
    return (x - m) / jnp.sqrt(v + eps)

def _scatter_add(tgt, idx, src, axis=0):
    return tgt.at[idx].add(src)

def _segment_sum(src, seg, n):
    return jax.ops.segment_sum(src, seg, n)
kernel_name = 'mk_macaron_d1_jaxref_r8_92c25e'

def setup_inputs(seed: int=0):
    np.random.seed(seed)
    _w = jnp.asarray

    def _L0_attn_setup():
        import jax, jax.numpy as jnp
        import numpy as np
        B, N, E = (4, 512, 256)
        H_DIM = 256
        HEADS = 16
        DH = H_DIM // HEADS
        LN_EPS = 1e-05

        def _heads(t):
            b, n, _ = t.shape
            return t.reshape(b, n, HEADS, DH).transpose(0, 2, 1, 3)

        def _layernorm(x, g, b):
            mu = jnp.mean(x, axis=-1, keepdims=True)
            var = jnp.mean(jnp.square(x - mu), axis=-1, keepdims=True)
            return (x - mu) * jax.lax.rsqrt(var + LN_EPS) * g + b
        key = jax.random.key(seed)
        ks = jax.random.split(key, 10)
        s = 1.0 / np.sqrt(E)
        so = 1.0 / np.sqrt(H_DIM)
        return {'x': jax.random.normal(ks[0], (B, N, E), jnp.float32), 'Wqk': jax.random.normal(ks[1], (E, H_DIM), jnp.float32) * s, 'bqk': jnp.zeros((H_DIM,), jnp.float32), 'Wv': jax.random.normal(ks[2], (E, H_DIM), jnp.float32) * s, 'bv': jnp.zeros((H_DIM,), jnp.float32), 'Wu': jax.random.normal(ks[3], (E, H_DIM), jnp.float32) * s, 'bu': jnp.zeros((H_DIM,), jnp.float32), 'Wo': jax.random.normal(ks[4], (H_DIM, E), jnp.float32) * so, 'bo': jnp.zeros((E,), jnp.float32), 'ln_g': jnp.ones((H_DIM,), jnp.float32), 'ln_b': jnp.zeros((H_DIM,), jnp.float32)}
    _L0_attn_in = _L0_attn_setup()

    def _L0_ffn_setup():
        import jax, jax.numpy as jnp
        import numpy as np
        from jax import lax
        B, S, H = (1, 256, 256)
        E, I, TOP_K = (64, 64, 8)
        SHARED_I = 64
        key = jax.random.key(seed)
        ks = jax.random.split(key, 8)
        sc = 0.02
        return {'hidden_states': jax.random.normal(ks[0], (B, S, H), jnp.float32), 'router_w': jax.random.normal(ks[1], (E, H), jnp.float32) * sc, 'gate_up_proj': jax.random.normal(ks[2], (E, 2 * I, H), jnp.float32) * sc, 'down_proj': jax.random.normal(ks[3], (E, H, I), jnp.float32) * sc, 'shared_gate_w': jax.random.normal(ks[4], (SHARED_I, H), jnp.float32) * sc, 'shared_up_w': jax.random.normal(ks[5], (SHARED_I, H), jnp.float32) * sc, 'shared_down_w': jax.random.normal(ks[6], (H, SHARED_I), jnp.float32) * sc, 'shared_expert_gate_w': jax.random.normal(ks[7], (1, H), jnp.float32) * sc}
    _L0_ffn_in = _L0_ffn_setup()
    _d = {'L0_attn_x': _L0_attn_in['x'], 'L0_attn_Wqk': _L0_attn_in['Wqk'], 'L0_attn_bqk': _L0_attn_in['bqk'], 'L0_attn_Wv': _L0_attn_in['Wv'], 'L0_attn_bv': _L0_attn_in['bv'], 'L0_attn_Wu': _L0_attn_in['Wu'], 'L0_attn_bu': _L0_attn_in['bu'], 'L0_attn_Wo': _L0_attn_in['Wo'], 'L0_attn_bo': _L0_attn_in['bo'], 'L0_attn_ln_g': _L0_attn_in['ln_g'], 'L0_attn_ln_b': _L0_attn_in['ln_b'], 'L0_ffn_router_w': _L0_ffn_in['router_w'], 'L0_ffn_gate_up_proj': _L0_ffn_in['gate_up_proj'], 'L0_ffn_down_proj': _L0_ffn_in['down_proj'], 'L0_ffn_shared_gate_w': _L0_ffn_in['shared_gate_w'], 'L0_ffn_shared_up_w': _L0_ffn_in['shared_up_w'], 'L0_ffn_shared_down_w': _L0_ffn_in['shared_down_w'], 'L0_ffn_shared_expert_gate_w': _L0_ffn_in['shared_expert_gate_w']}
    _x0 = _d['L0_attn_x']
    _d['L0_attn_x'] = jax.random.normal(jax.random.fold_in(jax.random.key(seed), 1), (8, 512, 256), dtype=_x0.dtype)
    del _x0
    return _d

def reference(L0_attn_x, L0_attn_Wqk, L0_attn_bqk, L0_attn_Wv, L0_attn_bv, L0_attn_Wu, L0_attn_bu, L0_attn_Wo, L0_attn_bo, L0_attn_ln_g, L0_attn_ln_b, L0_ffn_router_w, L0_ffn_gate_up_proj, L0_ffn_down_proj, L0_ffn_shared_gate_w, L0_ffn_shared_up_w, L0_ffn_shared_down_w, L0_ffn_shared_expert_gate_w):

    def _L0_attn_ref(x, Wqk, bqk, Wv, bv, Wu, bu, Wo, bo, ln_g, ln_b):
        import jax, jax.numpy as jnp
        import numpy as np
        B, N, E = (4, 512, 256)
        H_DIM = 256
        HEADS = 16
        DH = H_DIM // HEADS
        LN_EPS = 1e-05

        def _heads(t):
            b, n, _ = t.shape
            return t.reshape(b, n, HEADS, DH).transpose(0, 2, 1, 3)

        def _layernorm(x, g, b):
            mu = jnp.mean(x, axis=-1, keepdims=True)
            var = jnp.mean(jnp.square(x - mu), axis=-1, keepdims=True)
            return (x - mu) * jax.lax.rsqrt(var + LN_EPS) * g + b
        q = x @ Wqk + bqk
        k = x @ Wqk + bqk
        v = jax.nn.silu(x @ Wv + bv)
        u = jax.nn.silu(x @ Wu + bu)
        q = jax.nn.elu(_heads(q))
        kh = jax.nn.elu(_heads(k))
        vh = _heads(v)
        kv = jnp.einsum('bhnd,bhne->bhde', kh, vh)
        out = jnp.einsum('bhnd,bhde->bhne', q, kv)
        out = out.transpose(0, 2, 1, 3).reshape(x.shape[0], x.shape[1], H_DIM)
        out = _layernorm(out, ln_g, ln_b)
        out = u * out
        return out @ Wo + bo

    def _L0_ffn_ref(hidden_states, router_w, gate_up_proj, down_proj, shared_gate_w, shared_up_w, shared_down_w, shared_expert_gate_w):
        import jax, jax.numpy as jnp
        import numpy as np
        from jax import lax
        B, S, H = (1, 256, 256)
        E, I, TOP_K = (64, 64, 8)
        SHARED_I = 64
        b, s, h_dim = hidden_states.shape
        h = hidden_states.reshape(-1, h_dim)
        T = h.shape[0]
        shared = jnp.dot(jax.nn.silu(jnp.dot(h, shared_gate_w.T)) * jnp.dot(h, shared_up_w.T), shared_down_w.T)
        shared = jax.nn.sigmoid(jnp.dot(h, shared_expert_gate_w.T)) * shared
        logits = jnp.dot(h, router_w.T)
        probs = jax.nn.softmax(logits.astype(jnp.float32), axis=-1)
        top_vals, top_idx = lax.top_k(probs, TOP_K)
        top_vals = top_vals / jnp.sum(top_vals, axis=-1, keepdims=True)
        top_vals = top_vals.astype(h.dtype)
        comb = jnp.zeros((T, E), h.dtype).at[jnp.arange(T)[:, None], top_idx].add(top_vals)

        def body(acc, xs):
            wgu, wd, w_e = xs
            g, u = jnp.split(jnp.dot(h, wgu.T), 2, axis=-1)
            eo = jnp.dot(jax.nn.silu(g) * u, wd.T)
            return (acc + eo * w_e[:, None], None)
        expert_out, _ = lax.scan(body, jnp.zeros_like(h), (gate_up_proj, down_proj, comb.T))
        return (expert_out + shared).reshape(b, s, h_dim)
    x = L0_attn_x
    x = x + 0.5 * _L0_ffn_ref(_layernorm(x, axis=-1), L0_ffn_router_w, L0_ffn_gate_up_proj, L0_ffn_down_proj, L0_ffn_shared_gate_w, L0_ffn_shared_up_w, L0_ffn_shared_down_w, L0_ffn_shared_expert_gate_w)
    x = x + _L0_attn_ref(_layernorm(x, axis=-1), L0_attn_Wqk, L0_attn_bqk, L0_attn_Wv, L0_attn_bv, L0_attn_Wu, L0_attn_bu, L0_attn_Wo, L0_attn_bo, L0_attn_ln_g, L0_attn_ln_b)
    x = x + 0.5 * _L0_ffn_ref(_layernorm(x, axis=-1), L0_ffn_router_w, L0_ffn_gate_up_proj, L0_ffn_down_proj, L0_ffn_shared_gate_w, L0_ffn_shared_up_w, L0_ffn_shared_down_w, L0_ffn_shared_expert_gate_w)
    return x

_drawn_inputs = setup_inputs


def setup_inputs(seed=0):
    import zlib

    import numpy as np

    out = dict(_drawn_inputs(seed))
    spreads = {'L0_attn_bqk': (0.0, 0.1),
     'L0_attn_bv': (0.0, 0.1),
     'L0_attn_bu': (0.0, 0.1),
     'L0_attn_bo': (0.0, 0.1),
     'L0_attn_ln_g': (1.0, 0.2),
     'L0_attn_ln_b': (0.0, 0.1)}
    factors = {'L0_ffn_router_w': 8.0,
     'L0_ffn_gate_up_proj': 8.0,
     'L0_ffn_down_proj': 8.0,
     'L0_ffn_shared_gate_w': 8.0,
     'L0_ffn_shared_up_w': 8.0,
     'L0_ffn_shared_down_w': 8.0,
     'L0_ffn_shared_expert_gate_w': 8.0}
    for name, (base, spread) in spreads.items():
        noise = np.random.default_rng([zlib.crc32(name.encode()), seed]).standard_normal(out[name].shape)
        drawn = base * np.exp(spread * noise) if base else spread * noise
        out[name] = jnp.asarray(drawn.astype(out[name].dtype))
    for name, factor in factors.items():
        out[name] = (out[name] * factor).astype(out[name].dtype)
    return out
```

```python
from contextlib import ExitStack

import concourse.bass as bass
from concourse import mybir

ALU = mybir.AluOpType
ACT = mybir.ActivationFunctionType
F32 = mybir.dt.float32
F16 = mybir.dt.float16
U32 = mybir.dt.uint32
AX_X = mybir.AxisListType.X
RMAX = bass.bass_isa.ReduceOp.max

P = 128


def macaron_kernel(nc, x_in, gate_up, down, shared_gate_up, shared_down, router,
                   w_qvu, b_qvu, w_o, b_o, ln_g, ln_b, out):
    NCH, _, TT, H = x_in.shape
    CH = P * TT
    KH = H // P
    PAIRS = gate_up.shape[1]
    E = 2 * PAIRS
    I = P // 2
    R = E + 1
    HD = 16
    QVU = 3 * H
    UNITS = PAIRS + 1
    TOPK = 8
    EPS = 1e-5
    LOWEST = -3.0e38

    GU = KH * 2 * P
    GROUP = 2
    SHIFT = 2 * GROUP
    GROUPS = PAIRS // GROUP
    LOADS = 4

    CW = 13
    COMB_SCALE = 2.0 ** (-4 - 2 * CW)

    ctx = ExitStack()
    with ctx:
        def sb(name, shape, dt):
            return ctx.enter_context(nc.sbuf_tensor(name, shape, dt))

        def sem(name):
            return ctx.enter_context(nc.semaphore(name))

        x = sb("x", [P, NCH * TT, H], F32)
        wgu = sb("wgu", [P, (PAIRS + SHIFT) * GU], F32)
        wd = sb("wd", [P, (PAIRS + SHIFT) * H], F32)
        wgu16 = wgu[:, :].bitcast(F16)
        wd16 = wd[:, :].bitcast(F16)
        ws_gu = sb("ws_gu", [P, 2 * KH * P], F16)
        ws_d = sb("ws_d", [P, 2 * H], F16)
        rw = sb("rw", [P, KH, R], F32)
        ident = sb("ident", [P, P], F32)
        head_mask = sb("head_mask", [P, P], F32)
        minus_half = sb("minus_half", [P, TT], F32)
        sc = sb("sc", [P, 8], F32)
        wmax = sb("wmax", [P, 16], F32)
        stats = sb("stats", [P, TT, 6], F32)
        mean_var = sb("mean_var", [P, TT, 2], F32)
        var_eps = sb("var_eps", [P, TT], F32)
        rstd = sb("rstd", [P, TT], F32)
        xn = sb("xn", [P, TT, H], F32)
        xT = sb("xT", [P, KH, CH], F32)
        xT_hi = sb("xT_hi", [P, 2, KH, CH], F16)
        xT_lo = sb("xT_lo", [P, 2, KH, CH], F16)
        logits = sb("logits", [P, TT, R], F32)
        top = sb("top", [P, TT, TOPK], F32)
        replaced = sb("replaced", [P, TT, E], F32)
        expo = sb("expo", [P, TT, E], F32)
        shared_th = sb("shared_th", [P, TT], F32)
        top_sum = sb("top_sum", [P, TT], F32)
        top_rec = sb("top_rec", [P, TT], F32)
        comb = sb("comb", [P, TT, R], F32)
        combT = sb("combT", [P, 2, CH], F32)
        kv = sb("kv", [P, KH, P], F32)

        SCRATCH = 16 * CH
        scratch = sb("scratch", [P, SCRATCH], F32)
        at = [0]

        def part(n):
            at[0] += n
            assert at[0] <= SCRATCH
            return scratch[:, at[0] - n:at[0]]

        cb = [part(CH) for _ in range(4)]
        cb_s = part(CH)
        th = [part(CH) for _ in range(2)]
        th_s = part(CH)
        act = [part(CH) for _ in range(2)]
        act_s = part(CH)
        act_hi = [part(CH // 2).bitcast(F16) for _ in range(4)]
        act_lo = [part(CH // 2).bitcast(F16) for _ in range(4)]
        act_hi_s = part(CH // 2).bitcast(F16)
        act_lo_s = part(CH // 2).bitcast(F16)
        at[0] = 0
        z = part(TT * QVU).rearrange("p (j n) -> p j n", j=TT)
        ez = part(TT * QVU).rearrange("p (j n) -> p j n", j=TT)
        qT = part(KH * CH).rearrange("p (k n) -> p k n", k=KH)
        gT = part(KH * CH).rearrange("p (k n) -> p k n", k=KH)
        s_gu32 = scratch[:, 0:KH * P]
        s_d32 = scratch[:, KH * P:KH * P + H]
        w_att = wgu[:, PAIRS * GU:PAIRS * GU + KH * QVU].rearrange("p (k n) -> p k n", k=KH)
        w_oa = wgu[:, PAIRS * GU + KH * QVU:PAIRS * GU + KH * QVU + KH * H].rearrange(
            "p (k n) -> p k n", k=KH)
        assert SHIFT * GU >= KH * (QVU + H) and SHIFT * H >= H
        b_att = sb("b_att", [P, QVU], F32)
        g_row = wd[:, PAIRS * H:PAIRS * H + H]
        b_row = wd[:, PAIRS * H + H:PAIRS * H + 2 * H]
        bo_row = wd[:, PAIRS * H + 2 * H:PAIRS * H + 3 * H]

        combT_dram = nc.dram_tensor("combT_dram", (2, R, CH), F32, kind="Internal").ap()

        bank = [ctx.enter_context(nc.psum_tensor(f"bank{i}", [P, 512], F32)) for i in range(8)]
        gate_ps, up_ps, y_ps = bank[0:2], bank[2:4], bank[4:6]
        tr_ps = bank[6:8]
        shared_ps, router_ps, comb_ps = bank[6], bank[6], bank[7]

        x_loaded = sem("x_loaded")
        w_loaded = [sem(f"w_loaded{i}") for i in range(LOADS)]
        small_loaded = sem("small_loaded")
        att_loaded = sem("att_loaded")
        waits_apart = sem("waits_apart")
        consts = sem("consts")
        const_step = sem("const_step")
        wmax_parts = sem("wmax_parts")
        wmax_rows = sem("wmax_rows")
        wmax_all = sem("wmax_all")
        scale_step = sem("scale_step")
        scales_ready = sem("scales_ready")
        w_hi = sem("w_hi")
        w_lo = sem("w_lo")
        bn_done = sem("bn_done")
        stats_ready = sem("stats_ready")
        var_ready = sem("var_ready")
        rstd_ready = sem("rstd_ready")
        xn_ready = sem("xn_ready")
        xT_in_psum = sem("xT_in_psum")
        xT_ready = sem("xT_ready")
        xhi_ready = sem("xhi_ready")
        xlo_ready = sem("xlo_ready")
        router_in_psum = sem("router_in_psum")
        logits_ready = sem("logits_ready")
        top_done = sem("top_done")
        replaced_done = sem("replaced_done")
        shifted_ready = sem("shifted_ready")
        exp_ready = sem("exp_ready")
        comb_step = sem("comb_step")
        comb_ready = sem("comb_ready")
        comb_in_psum = sem("comb_in_psum")
        combT_ready = sem("combT_ready")
        combT_stored = sem("combT_stored")
        cb_loaded = [sem(f"cb_loaded{i}") for i in range(4)]
        cbs_loaded = sem("cbs_loaded")
        gu_ready = sem("gu_ready")
        th_ready = sem("th_ready")
        gated = sem("gated")
        prod_ready = sem("prod_ready")
        act_ready = sem("act_ready")
        hi_ready = sem("hi_ready")
        lo_ready = sem("lo_ready")
        down_done = sem("down_done")
        x_ready = sem("x_ready")
        out_stored = sem("out_stored")
        proj_in_psum = sem("proj_in_psum")
        z_ready = sem("z_ready")
        ez_ready = sem("ez_ready")
        em_ready = sem("em_ready")
        kvu_ready = sem("kvu_ready")
        kv_in_psum = sem("kv_in_psum")
        kv_ready = sem("kv_ready")
        kT_in_psum = sem("kT_in_psum")
        qT_ready = sem("qT_ready")
        o_in_psum = sem("o_in_psum")
        o_ready = sem("o_ready")
        o_bn = sem("o_bn")
        o_stats = sem("o_stats")
        o_var = sem("o_var")
        o_rstd = sem("o_rstd")
        o_norm = sem("o_norm")
        o_gain = sem("o_gain")
        o_bias = sem("o_bias")
        g_ready = sem("g_ready")
        gT_in_psum = sem("gT_in_psum")
        gT_ready = sem("gT_ready")
        xb_ready = sem("xb_ready")
        y_in_psum = sem("y_in_psum")
        x_mixed = sem("x_mixed")

        PRIME = 4

        def unit(ph, c, u):
            return PRIME + ph * NCH * UNITS + c * UNITS + u

        SHARED = 0

        PASSES = ((0, 0), (0, 1), (1, 0))

        def tiles(c):
            return x[:, bass.ds(c * TT, TT), :]

        def tile_of(c, j):
            return x[:, bass.ds(c * TT + j, 1), :].rearrange("p a n -> p (a n)")


        def gu32(g):
            return wgu[:, bass.ds((g * GROUP + SHIFT) * GU, GROUP * GU)].rearrange(
                "p (a n) -> p a n", a=GROUP)

        def d32(g):
            return wd[:, bass.ds((g * GROUP + SHIFT) * H, GROUP * H)].rearrange(
                "p (a n) -> p a n", a=GROUP)

        def gu_half(g, part_):
            return wgu16[:, bass.ds(g * GROUP * 2 * GU, GROUP * 2 * GU)].rearrange(
                "p (a s n) -> p a s n", a=GROUP, s=2)[:, :, part_, :]

        def d_half(g, part_):
            return wd16[:, bass.ds(g * GROUP * 2 * H, GROUP * 2 * H)].rearrange(
                "p (a s n) -> p a s n", a=GROUP, s=2)[:, :, part_, :]

        def apart(engine):
            engine.sem_inc(waits_apart, 1)

        block = ctx.enter_context(nc.Block())

        @block.sync
        def _(sp):
            sp.dma_start(x[:, :, :].rearrange("p (c j) h -> p c (j h)", c=NCH),
                         x_in.rearrange("c p j h -> p c (j h)")).then_inc(x_loaded, 16)
            sp.dma_start(rw[:, :, :], router).then_inc(small_loaded, 16)
            sp.dma_start(s_gu32, shared_gate_up).then_inc(small_loaded, 16)
            sp.dma_start(s_d32[64:128, :], shared_down).then_inc(small_loaded, 16)
            n = PAIRS // LOADS
            for i in range(LOADS):
                sp.dma_start(wgu[:, (SHIFT + i * n) * GU:(SHIFT + (i + 1) * n) * GU],
                             gate_up[:, i * n:(i + 1) * n, :].rearrange("p a n -> p (a n)")
                             ).then_inc(w_loaded[i], 16)
                sp.dma_start(wd[:, (SHIFT + i * n) * H:(SHIFT + (i + 1) * n) * H],
                             down[:, i * n:(i + 1) * n, :].rearrange("p a n -> p (a n)")
                             ).then_inc(w_loaded[i], 16)

            sp.wait_ge(w_lo, 2 + 2 * GROUPS + 2)
            sp.dma_start(w_att, w_qvu).then_inc(att_loaded, 16)
            sp.dma_start(w_oa, w_o).then_inc(att_loaded, 16)
            sp.dma_start(b_att[:, :], b_qvu.partition_broadcast(P)).then_inc(att_loaded, 16)
            for row, vec in ((g_row, ln_g), (b_row, ln_b), (bo_row, b_o)):
                sp.dma_start(row, vec.partition_broadcast(P)).then_inc(att_loaded, 16)

            def spread(dst, par, row, done):
                src = combT_dram[par, bass.ds(row, 1), :].rearrange("a n -> (a n)")
                sp.dma_start(dst, src.partition_broadcast(I)).then_inc(done, 16)

            def pair(ph, c, u, par, i):
                sp.wait_ge(act_ready, unit(ph, c, u) - 3)
                spread(cb[i][0:I, :], par, 2 * (u - 1), cb_loaded[i])
                spread(cb[i][I:P, :], par, 2 * (u - 1) + 1, cb_loaded[i])

            def chunk(ph, c, par, store_last=False):
                sp.wait_ge(combT_ready, ph * NCH + c + 1)
                sp.dma_start(combT_dram[par, :, :], combT[0:R, par, :]).then_inc(combT_stored, 16)
                sp.wait_ge(combT_stored, 16 * (ph * NCH + c + 1))
                spread(cb_s[I:P, :], par, E, cbs_loaded)
                for i in range(4):
                    pair(ph, c, i + 1, par, i)
                if store_last:
                    store(c - 1)
                with sp.Fori(1, PAIRS // 4) as q:
                    for i in range(4):
                        pair(ph, c, 4 * q + i + 1, par, i)

            def store(c):
                sp.wait_ge(x_ready, NCH + c + 2)
                sp.dma_start(out[bass.ds(c, 1), :, :, :].rearrange("a p j h -> p (a j h)"),
                             tiles(c).rearrange("p j h -> p (j h)")).then_inc(out_stored, 16)

            with sp.Fori(0, NCH // 2) as cc:
                chunk(0, 2 * cc, 0)
                chunk(0, 2 * cc + 1, 1)
            chunk(1, 0, 0)
            chunk(1, 1, 1, True)
            with sp.Fori(1, NCH // 2) as cc:
                chunk(1, 2 * cc, 0, True)
                chunk(1, 2 * cc + 1, 1, True)
            store(NCH - 1)
            sp.wait_ge(out_stored, 16 * NCH)

        @block.gpsimd
        def _(pool):
            nc.gpsimd.memset(ident[:, :], 0.0).then_inc(const_step, 1)
            nc.gpsimd.memset(head_mask[:, :], 0.5).then_inc(const_step, 1)
            nc.gpsimd.memset(minus_half[:, :], -0.5).then_inc(consts, 1)
            pool.wait_ge(const_step, 2)
            nc.gpsimd.affine_select(out=ident[:, :], in_=ident[:, :], compare_op=ALU.not_equal, fill=1.0,
                                    base=0, pattern=[[-1, P]], channel_multiplier=1).then_inc(consts, 1)
            heads = head_mask[:, :].rearrange("p (a d) -> p a d", d=HD)
            nc.gpsimd.affine_select(out=heads, in_=heads, compare_op=ALU.is_ge, fill=0.0, base=0,
                                    pattern=[[-HD, P // HD], [0, HD]], channel_multiplier=1
                                    ).then_inc(const_step, 1)
            pool.wait_ge(const_step, 3)
            nc.gpsimd.affine_select(out=heads, in_=heads, compare_op=ALU.is_ge, fill=0.0, base=HD - 1,
                                    pattern=[[HD, P // HD], [0, HD]], channel_multiplier=-1
                                    ).then_inc(consts, 1)
            pool.sem_inc(act_ready, PRIME)

            def ln_rstd(n):
                pool.wait_ge(stats_ready, TT * (n + 1))
                apart(pool)
                nc.gpsimd.tensor_scalar(var_eps[:, :], mean_var[:, :, 1], EPS, None, ALU.add
                                        ).then_inc(var_ready, 1)
                pool.wait_ge(var_ready, n + 1)
                nc.gpsimd.tensor_tensor(rstd[:, :], var_eps[:, :], minus_half[:, :], ALU.pow
                                        ).then_inc(rstd_ready, 1)

            def weigh(w, buf, weights):
                pool.wait_ge(prod_ready, w + 1)
                nc.gpsimd.tensor_tensor(buf, buf, weights, ALU.mult).then_inc(act_ready, 1)

            def pair(ph, c, u, q, i):
                pool.wait_ge(cb_loaded[i], 32 * ((ph * NCH + c) * (PAIRS // 4) + q + 1))
                weigh(unit(ph, c, u), act[i % 2], cb[i])

            def pairs_of(ph, c, q):
                for i in range(4):
                    pair(ph, c, 4 * q + 3 + i, q + (2 + i) // 4, (2 + i) % 4)

            def pairs(ph, c, q0, q1):
                with pool.Fori(q0, q1) as q:
                    pairs_of(ph, c, q)

            def chunk(ph, c, par, nxt):
                pool.wait_ge(cbs_loaded, 16 * (ph * NCH + c + 1))
                pool.wait_ge(act_ready, unit(ph, c, SHARED))
                weigh(unit(ph, c, SHARED), act_s[I:P, :], cb_s[I:P, :])
                pool.wait_ge(act_ready, unit(ph, c, SHARED) + 1)
                if nxt:
                    ln_rstd(2 * ph * NCH + c + 1)
                pair(ph, c, 1, 0, 0)
                pair(ph, c, 2, 0, 1)
                pairs(ph, c, 0, 2)
                pairs(ph, c, 2, 4)
                pairs(ph, c, 4, 6)
                pairs_of(ph, c, 6)
                pair(ph, c, PAIRS - 1, PAIRS // 4 - 1, 2)
                pair(ph, c, PAIRS, PAIRS // 4 - 1, 3)

            def mixture(ph):
                ln_rstd(2 * ph * NCH)
                if ph == 0:
                    pool.wait_ge(wmax_rows, 2)
                    nc.gpsimd.partition_all_reduce(wmax[:, 14:16], wmax[:, 12:14], P, RMAX
                                                   ).then_inc(wmax_all, 1)
                with pool.Fori(0, NCH // 2 - 1) as cc:
                    chunk(ph, 2 * cc, 0, True)
                    chunk(ph, 2 * cc + 1, 1, True)
                chunk(ph, NCH - 2, 0, True)
                chunk(ph, NCH - 1, 1, False)

            def attention():
                pool.wait_ge(att_loaded, 6 * 16)
                with pool.Fori(0, NCH) as b:
                    ln_rstd(NCH + b)
                    pool.wait_ge(ez_ready, 2 * b + 1)
                    apart(pool)
                    nc.gpsimd.tensor_scalar(ez[:, :, 0:H], ez[:, :, 0:H], 1.0, -1.0, ALU.min, ALU.add
                                            ).then_inc(em_ready, 1)
                    pool.wait_ge(o_stats, TT * (b + 1))
                    apart(pool)
                    nc.gpsimd.tensor_scalar(var_eps[:, :], mean_var[:, :, 1], EPS, None, ALU.add
                                            ).then_inc(o_var, 1)
                    pool.wait_ge(o_var, b + 1)
                    nc.gpsimd.tensor_tensor(rstd[:, :], var_eps[:, :], minus_half[:, :], ALU.pow
                                            ).then_inc(o_rstd, 1)
                    pool.wait_ge(xT_in_psum, NCH + b + 1)
                    nc.gpsimd.tensor_tensor(xn[:, :, :], tiles(b),
                                            bo_row[:, None, :].broadcast_to([P, TT, H]), ALU.add
                                            ).then_inc(xb_ready, 1)

            mixture(0)
            attention()
            mixture(1)

        @block.scalar
        def _(act_e):
            act_e.sem_inc(th_ready, PRIME)
            act_e.sem_inc(hi_ready, PRIME)
            act_e.sem_inc(w_hi, 2)

            def split_hi(n, out, in_, scale):
                act_e.wait_ge(w_lo, n)
                nc.scalar.activation(out, in_, ACT.Copy, scale=scale).then_inc(w_hi, 1)

            def xT_out(n, m, par):
                act_e.wait_ge(xT_in_psum, n + 1)
                if not (isinstance(m, int) and m == 0):
                    act_e.wait_ge(router_in_psum, m)
                for k in range(KH):
                    nc.scalar.activation(xT[:, k, :], tr_ps[k][:, :], ACT.Copy).then_inc(xT_ready, 1)
                for k in range(KH):
                    nc.scalar.activation(xT_hi[:, par, k, :], tr_ps[k][:, :], ACT.Copy
                                         ).then_inc(xhi_ready, 1)

            def logits_out(m):
                act_e.wait_ge(router_in_psum, m + 1)
                nc.scalar.activation(logits[:, :, :].rearrange("p j n -> p (j n)"),
                                     router_ps[:, 0:TT * R], ACT.Copy).then_inc(logits_ready, 1)

            def router_exp(m):
                act_e.wait_ge(shifted_ready, m + 1)
                nc.scalar.activation(expo[:, :, :], expo[:, :, :], ACT.Exp).then_inc(exp_ready, 1)
                nc.scalar.activation(shared_th[:, :], logits[:, :, E], ACT.Tanh, scale=0.5
                                     ).then_inc(exp_ready, 1)

            def comb_out(m, par):
                act_e.wait_ge(comb_in_psum, m + 1)
                nc.scalar.activation(combT[0:R, par, :], comb_ps[0:R, :], ACT.Copy, scale=COMB_SCALE
                                     ).then_inc(combT_ready, 1)

            def tanh(w, out, ps):
                act_e.wait_ge(gu_ready, 2 * w + 1)
                act_e.wait_ge(gated, w - 1)
                nc.scalar.activation(out, ps, ACT.Tanh, scale=sc[0:out.shape[0], 4:5]).then_inc(th_ready, 1)

            def hi(w, out, buf):
                act_e.wait_ge(act_ready, w + 1)
                act_e.wait_ge(down_done, w - 3)
                nc.scalar.activation(out, buf, ACT.Copy).then_inc(hi_ready, 1)

            def pair(ph, c, u, i, before):
                tanh(unit(ph, c, u), th[i % 2], gate_ps[i % 2][:, :])
                hi(unit(ph, c, u) - 1, act_hi[before], act[before % 2])

            def pairs_of(ph, c, q):
                for i in range(4):
                    pair(ph, c, 4 * q + 3 + i, (2 + i) % 4, (1 + i) % 4)

            def pairs(ph, c, q0, q1):
                with act_e.Fori(q0, q1) as q:
                    pairs_of(ph, c, q)

            def chunk(ph, c, par, nxt):
                n, m = 2 * ph * NCH + c + 1, ph * NCH + c + 1
                tanh(unit(ph, c, SHARED), th_s[0:I, :], shared_ps[0:I, :])
                tanh(unit(ph, c, 1), th[0], gate_ps[0][:, :])
                hi(unit(ph, c, SHARED), act_hi_s[I:P, :], act_s[I:P, :])
                pair(ph, c, 2, 1, 0)
                pairs(ph, c, 0, 2)
                if nxt:
                    xT_out(n, m, 1 - par)
                pairs(ph, c, 2, 4)
                if nxt:
                    logits_out(m)
                pairs(ph, c, 4, 6)
                if nxt:
                    router_exp(m)
                pairs_of(ph, c, 6)
                if nxt:
                    comb_out(m, 1 - par)
                pair(ph, c, PAIRS - 1, 2, 1)
                pair(ph, c, PAIRS, 3, 2)
                hi(unit(ph, c, PAIRS), act_hi[3], act[1])

            def mixture(ph):
                xT_out(2 * ph * NCH, ph * NCH, 0)
                logits_out(ph * NCH)
                router_exp(ph * NCH)
                comb_out(ph * NCH, 0)
                if ph == 0:
                    act_e.wait_ge(scales_ready, 1)
                    split_hi(2, ws_gu[:, 0:KH * P], s_gu32, sc[:, 2:3])
                    split_hi(2, ws_d[I:P, 0:H], s_d32[I:P, :], sc[I:P, 3:4])
                    with act_e.Fori(0, GROUPS) as g:
                        split_hi(2 * g + 2, gu_half(g, 0), gu32(g), sc[:, 2:3])
                        split_hi(2 * g + 3, d_half(g, 0), d32(g), sc[:, 3:4])
                with act_e.Fori(0, NCH // 2 - 1) as cc:
                    chunk(ph, 2 * cc, 0, True)
                    chunk(ph, 2 * cc + 1, 1, True)
                chunk(ph, NCH - 2, 0, True)
                chunk(ph, NCH - 1, 1, False)

            def attention():
                with act_e.Fori(0, NCH) as b:
                    act_e.wait_ge(xT_in_psum, NCH + b + 1)
                    for k in range(KH):
                        nc.scalar.activation(xT[:, k, :], tr_ps[k][:, :], ACT.Copy).then_inc(xT_ready, 1)
                    act_e.wait_ge(z_ready, 2 * TT * (b + 1))
                    nc.scalar.activation(ez[:, :, 0:H], z[:, :, 0:H], ACT.Exp).then_inc(ez_ready, 1)
                    nc.scalar.activation(ez[:, :, H:QVU], z[:, :, H:QVU], ACT.Tanh, scale=0.5
                                         ).then_inc(ez_ready, 1)
                    act_e.wait_ge(kT_in_psum, b + 1)
                    for k in range(KH):
                        nc.scalar.activation(qT[:, k, :], tr_ps[k][:, :], ACT.Copy).then_inc(qT_ready, 1)
                    act_e.wait_ge(o_in_psum, b + 1)
                    for h in range(2):
                        nc.scalar.activation(ez[:, 2 * h:2 * h + 2, 0:H],
                                             y_ps[h][:, :].rearrange("p (j n) -> p j n", j=2), ACT.Copy
                                             ).then_inc(o_ready, 1)
                    act_e.wait_ge(gT_in_psum, b + 1)
                    for k in range(KH):
                        nc.scalar.activation(gT[:, k, :], tr_ps[k][:, :], ACT.Copy).then_inc(gT_ready, 1)

            mixture(0)
            attention()
            mixture(1)

        @block.vector
        def _(dve):
            for s in (gated, prod_ready, lo_ready):
                dve.sem_inc(s, PRIME)
            dve.sem_inc(x_ready, 1)
            dve.sem_inc(x_mixed, 1)
            dve.sem_inc(w_lo, 2)

            def ln_stats(n, c, updated, count):
                dve.wait_ge(updated, count)
                for j in range(TT):
                    nc.vector.bn_stats(stats[:, j, :], tile_of(c, j)).then_inc(bn_done, 1)
                dve.wait_ge(bn_done, TT * (n + 1))
                apart(dve)
                for j in range(TT):
                    nc.vector.bn_aggr(mean_var[:, j, :], stats[:, j, :]).then_inc(stats_ready, 1)

            def ln_apply(n, c):
                dve.wait_ge(rstd_ready, n + 1)
                for j in range(TT):
                    i = nc.vector.tensor_scalar(xn[:, j, :], tile_of(c, j), mean_var[:, j, 0:1],
                                                rstd[:, j:j + 1], ALU.subtract, ALU.mult)
                i.then_inc(xn_ready, 1)

            def xT_low(m, par):
                dve.wait_ge(xhi_ready, KH * (m + 1))
                for k in range(KH):
                    nc.vector.tensor_tensor(xT_lo[:, par, k, :], tr_ps[k][:, :], xT_hi[:, par, k, :],
                                            ALU.subtract).then_inc(xlo_ready, 1)

            def router_top(m):
                dve.wait_ge(logits_ready, m + 1)
                apart(dve)
                for j in range(TT):
                    nc.vector.max(top[:, j, :], logits[:, j, 0:E]).then_inc(top_done, 1)
                dve.wait_ge(top_done, TT * (m + 1))
                apart(dve)
                for j in range(TT):
                    nc.vector.match_replace(replaced[:, j, :], top[:, j, :], logits[:, j, 0:E], LOWEST
                                            ).then_inc(replaced_done, 1)
                nc.vector.tensor_tensor(expo[:, :, :], logits[:, :, 0:E],
                                        top[:, :, 0:1].broadcast_to([P, TT, E]), ALU.subtract
                                        ).then_inc(shifted_ready, 1)
                dve.wait_ge(replaced_done, TT * (m + 1))
                nc.vector.tensor_tensor(replaced[:, :, :], logits[:, :, 0:E], replaced[:, :, :],
                                        ALU.not_equal).then_inc(comb_step, 1)

            def router_weights(m):
                dve.wait_ge(exp_ready, 2 * (m + 1))
                dve.wait_ge(comb_step, 4 * m + 1)
                nc.vector.tensor_tensor(expo[:, :, :], expo[:, :, :], replaced[:, :, :], ALU.mult
                                        ).then_inc(comb_step, 1)
                dve.wait_ge(comb_step, 4 * m + 2)
                nc.vector.reduce_sum(top_sum[:, :], expo[:, :, :], AX_X).then_inc(comb_step, 1)
                dve.wait_ge(comb_step, 4 * m + 3)
                nc.vector.reciprocal(top_rec[:, :], top_sum[:, :]).then_inc(comb_step, 1)
                nc.vector.tensor_scalar(comb[:, :, E], shared_th[:, :], 0.5, 0.5, ALU.mult, ALU.add
                                        ).then_inc(comb_ready, 1)
                dve.wait_ge(comb_step, 4 * m + 4)
                nc.vector.tensor_tensor(comb[:, :, 0:E], expo[:, :, :],
                                        top_rec[:, :, None].broadcast_to([P, TT, E]), ALU.mult
                                        ).then_inc(comb_ready, 1)

            def gate(w, buf, gate_in, up_in, th_in, buf_up=None):
                dve.wait_ge(lo_ready, w - 1)
                dve.wait_ge(th_ready, w + 1)
                nc.vector.scalar_tensor_tensor(out=buf, in0=th_in, scalar=1.0, in1=gate_in,
                                               op0=ALU.add, op1=ALU.mult).then_inc(gated, 1)
                dve.wait_ge(gu_ready, 2 * w + 2)
                dve.wait_ge(gated, w + 1)
                nc.vector.tensor_tensor(buf, buf, up_in, ALU.mult).then_inc(prod_ready, 1)

            def low(w, out, buf, hi_in):
                dve.wait_ge(hi_ready, w + 1)
                nc.vector.tensor_tensor(out, buf, hi_in, ALU.subtract).then_inc(lo_ready, 1)

            def low_s(w):
                low(w, act_lo_s[I:P, :], act_s[I:P, :], act_hi_s[I:P, :])

            def gate_pair(w, i):
                gate(w, act[i % 2], gate_ps[i % 2][:, :], up_ps[i % 2][:, :], th[i % 2])

            def pair(ph, c, u, i, before):
                gate_pair(unit(ph, c, u), i)
                low(unit(ph, c, u) - 1, act_lo[before], act[before % 2], act_hi[before])

            def pairs_of(ph, c, q):
                for i in range(4):
                    pair(ph, c, 4 * q + 3 + i, (2 + i) % 4, (1 + i) % 4)

            def pairs(ph, c, q0, q1):
                with dve.Fori(q0, q1) as q:
                    pairs_of(ph, c, q)

            def chunk(ph, c, par, nxt):
                n, m = 2 * ph * NCH + c + 1, ph * NCH + c + 1
                gate(unit(ph, c, SHARED), act_s[I:P, :], shared_ps[0:I, :], shared_ps[I:P, :], th_s[0:I, :])
                if nxt:
                    if ph == 0:
                        ln_stats(n, c + 1, x_loaded, 16)
                    else:
                        ln_stats(n, c + 1, x_mixed, NCH + 1)
                gate_pair(unit(ph, c, 1), 0)
                low_s(unit(ph, c, SHARED))
                pair(ph, c, 2, 1, 0)
                if nxt:
                    ln_apply(n, c + 1)
                pairs(ph, c, 0, 2)
                if nxt:
                    xT_low(m, 1 - par)
                pairs(ph, c, 2, 4)
                if nxt:
                    router_top(m)
                pairs(ph, c, 4, 6)
                if nxt:
                    router_weights(m)
                pairs_of(ph, c, 6)
                pair(ph, c, PAIRS - 1, 2, 1)
                pair(ph, c, PAIRS, 3, 2)
                low(unit(ph, c, PAIRS), act_lo[3], act[1], act_hi[3])
                dve.wait_ge(down_done, unit(ph, c, PAIRS) + 1)
                for h in range(2):
                    rows = x[:, bass.ds(c * TT + 2 * h, 2), :].rearrange("p a n -> p (a n)")
                    i = nc.vector.scalar_tensor_tensor(out=rows, in0=y_ps[h][:, :], scalar=sc[:, 5:6],
                                                       in1=rows, op0=ALU.mult, op1=ALU.add)
                i.then_inc(x_ready, 1)

            def ready_first(ph):
                n, m = 2 * ph * NCH, ph * NCH
                if ph == 0:
                    ln_stats(n, 0, x_loaded, 16)
                else:
                    ln_stats(n, 0, x_mixed, NCH + 1)
                ln_apply(n, 0)
                xT_low(m, 0)
                router_top(m)
                router_weights(m)

            def split_lo(n, out, in_, scale, hi_in):
                dve.wait_ge(w_hi, n + 1)
                nc.vector.scalar_tensor_tensor(out=out, in0=in_, scalar=scale, in1=hi_in,
                                               op0=ALU.mult, op1=ALU.subtract).then_inc(w_lo, 1)

            def weight_scales():
                dve.wait_ge(small_loaded, 48)
                nc.vector.memset(wmax[:, 9:12], 0.0).then_inc(wmax_parts, 1)
                dve.wait_ge(wmax_parts, 1)
                nc.vector.tensor_reduce(wmax[:, 4:5], s_gu32, AX_X, ALU.max, apply_absolute_value=True
                                        ).then_inc(wmax_parts, 1)
                nc.vector.tensor_reduce(wmax[I:P, 9:10], s_d32[I:P, :], AX_X, ALU.max,
                                        apply_absolute_value=True).then_inc(wmax_parts, 1)
                n = PAIRS // LOADS
                for i in range(LOADS):
                    dve.wait_ge(w_loaded[i], 32)
                    nc.vector.tensor_reduce(wmax[:, i:i + 1],
                                            wgu[:, (SHIFT + i * n) * GU:(SHIFT + (i + 1) * n) * GU],
                                            AX_X, ALU.max, apply_absolute_value=True).then_inc(wmax_parts, 1)
                    nc.vector.tensor_reduce(wmax[:, 5 + i:6 + i],
                                            wd[:, (SHIFT + i * n) * H:(SHIFT + (i + 1) * n) * H],
                                            AX_X, ALU.max, apply_absolute_value=True).then_inc(wmax_parts, 1)
                dve.wait_ge(wmax_parts, 3 + 2 * LOADS)
                nc.vector.tensor_reduce(wmax[:, 12:13], wmax[:, 0:5], AX_X, ALU.max).then_inc(wmax_rows, 1)
                nc.vector.tensor_reduce(wmax[:, 13:14], wmax[:, 5:10], AX_X, ALU.max).then_inc(wmax_rows, 1)
                dve.wait_ge(wmax_all, 1)
                bits = sc[:, :].bitcast(U32)
                nc.vector.tensor_scalar(bits[:, 0:2], wmax[:, 14:16].bitcast(U32), 0x7F800000, None,
                                        ALU.bitwise_and).then_inc(scale_step, 1)
                dve.wait_ge(scale_step, 1)
                nc.vector.tensor_scalar(sc[:, 0:2], sc[:, 0:2], 2.0 ** -63, None, ALU.max
                                        ).then_inc(scale_step, 1)
                dve.wait_ge(scale_step, 2)
                nc.vector.tensor_scalar(bits[:, 2:4], bits[:, 0:2], -1.0, float((254 + CW) << 23),
                                        ALU.mult, ALU.add).then_inc(scale_step, 1)
                nc.vector.tensor_scalar(sc[:, 4:5], sc[:, 0:1], 2.0 ** (-CW - 1), None, ALU.mult
                                        ).then_inc(scale_step, 1)
                nc.vector.tensor_scalar(sc[:, 6:7], sc[:, 0:1], sc[:, 0:1], 2.0 ** (2 - CW),
                                        ALU.mult, ALU.mult).then_inc(scale_step, 1)
                dve.wait_ge(scale_step, 5)
                nc.vector.tensor_scalar(sc[:, 5:6], sc[:, 6:7], sc[:, 1:2], None, ALU.mult
                                        ).then_inc(scale_step, 1)
                dve.wait_ge(scale_step, 6)
                dve.sem_inc(scales_ready, 1)
                split_lo(2, ws_gu[:, KH * P:2 * KH * P], s_gu32, sc[:, 2:3], ws_gu[:, 0:KH * P])
                split_lo(3, ws_d[I:P, H:2 * H], s_d32[I:P, :], sc[I:P, 3:4], ws_d[I:P, 0:H])
                with dve.Fori(0, GROUPS) as g:
                    split_lo(2 * g + 4, gu_half(g, 1), gu32(g), sc[:, 2:3], gu_half(g, 0))
                    split_lo(2 * g + 5, d_half(g, 1), d32(g), sc[:, 3:4], d_half(g, 0))

            def mixture(ph):
                ready_first(ph)
                if ph == 0:
                    weight_scales()
                with dve.Fori(0, NCH // 2 - 1) as cc:
                    chunk(ph, 2 * cc, 0, True)
                    chunk(ph, 2 * cc + 1, 1, True)
                chunk(ph, NCH - 2, 0, True)
                chunk(ph, NCH - 1, 1, False)

            def attention():
                dve.wait_ge(att_loaded, 6 * 16)
                with dve.Fori(0, NCH) as b:
                    ln_stats(NCH + b, b, x_ready, NCH + 1)
                    ln_apply(NCH + b, b)
                    for j in range(TT):
                        dve.wait_ge(proj_in_psum, 2 * (TT * b + j) + 1)
                        nc.vector.tensor_tensor(z[:, j, 0:2 * H], bank[j % 2][:, :], b_att[:, 0:2 * H],
                                                ALU.add).then_inc(z_ready, 1)
                        dve.wait_ge(proj_in_psum, 2 * (TT * b + j) + 2)
                        nc.vector.tensor_tensor(z[:, j, 2 * H:QVU], bank[2 + j % 2][:, 0:H],
                                                b_att[:, 2 * H:QVU], ALU.add).then_inc(z_ready, 1)
                    dve.wait_ge(em_ready, b + 1)
                    nc.vector.scalar_tensor_tensor(out=z[:, :, 0:H], in0=z[:, :, 0:H], scalar=0.0,
                                                   in1=ez[:, :, 0:H], op0=ALU.max, op1=ALU.add
                                                   ).then_inc(kvu_ready, 1)
                    dve.wait_ge(ez_ready, 2 * b + 2)
                    nc.vector.scalar_tensor_tensor(out=z[:, :, H:QVU], in0=ez[:, :, H:QVU], scalar=1.0,
                                                   in1=z[:, :, H:QVU], op0=ALU.add, op1=ALU.mult
                                                   ).then_inc(kvu_ready, 1)
                    dve.wait_ge(kv_in_psum, b + 1)
                    nc.vector.tensor_tensor(kv[:, :, :],
                                            bank[0][:, 0:KH * P].rearrange("p (k n) -> p k n", k=KH),
                                            head_mask[:, None, :].broadcast_to([P, KH, P]), ALU.mult
                                            ).then_inc(kv_ready, 1)
                    dve.wait_ge(o_ready, 2 * (b + 1))
                    for j in range(TT):
                        nc.vector.bn_stats(stats[:, j, :], ez[:, j, 0:H]).then_inc(o_bn, 1)
                    dve.wait_ge(o_bn, TT * (b + 1))
                    apart(dve)
                    for j in range(TT):
                        nc.vector.bn_aggr(mean_var[:, j, :], stats[:, j, :]).then_inc(o_stats, 1)
                    dve.wait_ge(o_rstd, b + 1)
                    for j in range(TT):
                        nc.vector.tensor_scalar(ez[:, j, 0:H], ez[:, j, 0:H], mean_var[:, j, 0:1],
                                                rstd[:, j:j + 1], ALU.subtract, ALU.mult
                                                ).then_inc(o_norm, 1)
                    o = ez[:, :, 0:H]
                    dve.wait_ge(o_norm, TT * (b + 1))
                    nc.vector.tensor_tensor(o, o, g_row[:, None, :].broadcast_to([P, TT, H]), ALU.mult
                                            ).then_inc(o_gain, 1)
                    dve.wait_ge(o_gain, b + 1)
                    nc.vector.tensor_tensor(o, o, b_row[:, None, :].broadcast_to([P, TT, H]), ALU.add
                                            ).then_inc(o_bias, 1)
                    dve.wait_ge(o_bias, b + 1)
                    nc.vector.scalar_tensor_tensor(out=o, in0=o, scalar=0.5, in1=z[:, :, 2 * H:QVU],
                                                   op0=ALU.mult, op1=ALU.mult).then_inc(g_ready, 1)
                    dve.wait_ge(y_in_psum, b + 1)
                    dve.wait_ge(xb_ready, b + 1)
                    for h in range(2):
                        rows = x[:, bass.ds(b * TT + 2 * h, 2), :].rearrange("p a n -> p (a n)")
                        i = nc.vector.tensor_tensor(
                            rows, y_ps[h][:, :],
                            xn[:, 2 * h:2 * h + 2, :].rearrange("p a n -> p (a n)"), ALU.add)
                    i.then_inc(x_mixed, 1)

            mixture(0)
            attention()
            mixture(1)

        @block.tensor
        def _(pe):
            pe.sem_inc(gu_ready, 2 * PRIME)
            pe.sem_inc(down_done, PRIME)

            def transpose_x(n):
                pe.wait_ge(xn_ready, n + 1)
                for k in range(KH):
                    for j in range(TT):
                        i = nc.tensor.transpose(tr_ps[k][:, j * P:(j + 1) * P],
                                                xn[:, j, k * P:(k + 1) * P], ident[:, :])
                i.then_inc(xT_in_psum, 1)

            def route(n, m):
                pe.wait_ge(xT_ready, KH * (n + 1))
                pe.wait_ge(xlo_ready, KH * (m + 1))
                for j in range(TT):
                    for k in range(KH):
                        i = nc.tensor.matmul(router_ps[:, j * R:(j + 1) * R],
                                             xT[:, k, j * P:(j + 1) * P], rw[:, k, :],
                                             start=(k == 0), stop=(k == KH - 1))
                i.then_inc(router_in_psum, 1)

            def transpose_comb(m):
                pe.wait_ge(comb_ready, 2 * (m + 1))
                for j in range(TT):
                    i = nc.tensor.transpose(comb_ps[0:R, j * P:(j + 1) * P], comb[:, j, :], ident[:, :])
                i.then_inc(comb_in_psum, 1)

            def gate_up_shared(w, par):
                for k in range(KH):
                    for n, (a, b) in enumerate(PASSES):
                        mv = (xT_hi, xT_lo)[b]
                        i = nc.tensor.matmul(shared_ps[:, :], ws_gu[:, (a * KH + k) * P:(a * KH + k + 1) * P],
                                             mv[:, par, k, :], start=(k + n == 0),
                                             stop=(k == KH - 1 and n == len(PASSES) - 1))
                i.then_inc(gu_ready, 2)

            def gate_up_pair(w, u, i4, par):
                pe.wait_ge(prod_ready, w - 1)
                for t, ps in ((0, gate_ps[i4 % 2]), (1, up_ps[i4 % 2])):
                    for k in range(KH):
                        for n, (a, b) in enumerate(PASSES):
                            mv = (xT_hi, xT_lo)[b]
                            i = nc.tensor.matmul(
                                ps[:, :], wgu16[:, bass.ds((u - 1) * 2 * GU + a * GU + (k * 2 + t) * P, P)],
                                mv[:, par, k, :], start=(k + n == 0),
                                stop=(k == KH - 1 and n == len(PASSES) - 1))
                    i.then_inc(gu_ready, 1)

            def down_product(w, hi_, lo_, wts, first, last):
                pe.wait_ge(hi_ready, w + 1)
                pe.wait_ge(lo_ready, w + 1)
                for j in range(TT):
                    for n, (a, b) in enumerate(PASSES):
                        i = nc.tensor.matmul(y_ps[j // 2][:, (j % 2) * H:(j % 2 + 1) * H],
                                             (hi_, lo_)[b][:, j * P:(j + 1) * P], wts(a),
                                             start=(first and j % 2 == 0 and n == 0),
                                             stop=(last and j % 2 == 1 and n == len(PASSES) - 1),
                                             skip_group_check=True)
                i.then_inc(down_done, 1)

            def down_shared(w):
                down_product(w, act_hi_s[I:P, :], act_lo_s[I:P, :],
                             lambda a: ws_d[I:P, a * H:(a + 1) * H], True, False)

            def down_pair(w, u, i4, last=False):
                down_product(w, act_hi[i4], act_lo[i4],
                             lambda a: wd16[:, bass.ds((u - 1) * 2 * H + a * H, H)], False, last)

            def pairs_of(ph, c, q, par):
                for i in range(4):
                    u = 4 * q + 3 + i
                    gate_up_pair(unit(ph, c, u), u, 2 + i, par)
                    down_pair(unit(ph, c, u - 2), u - 2, i)

            def pairs(ph, c, q0, q1, par):
                with pe.Fori(q0, q1) as q:
                    pairs_of(ph, c, q, par)

            def chunk(ph, c, par, nxt):
                n, m = 2 * ph * NCH + c + 1, ph * NCH + c + 1
                gate_up_shared(unit(ph, c, SHARED), par)
                gate_up_pair(unit(ph, c, 1), 1, 0, par)
                gate_up_pair(unit(ph, c, 2), 2, 1, par)
                pe.wait_ge(x_ready, ph * NCH + c + 1)
                down_shared(unit(ph, c, SHARED))
                pairs(ph, c, 0, 2, par)
                if nxt:
                    transpose_x(n)
                pairs(ph, c, 2, 4, par)
                if nxt:
                    route(n, m)
                pairs(ph, c, 4, 6, par)
                pairs_of(ph, c, 6, par)
                if nxt:
                    transpose_comb(m)
                gate_up_pair(unit(ph, c, PAIRS - 1), PAIRS - 1, 2, par)
                down_pair(unit(ph, c, PAIRS - 3), PAIRS - 3, 0)
                gate_up_pair(unit(ph, c, PAIRS), PAIRS, 3, par)
                down_pair(unit(ph, c, PAIRS - 2), PAIRS - 2, 1)
                down_pair(unit(ph, c, PAIRS - 1), PAIRS - 1, 2)
                down_pair(unit(ph, c, PAIRS), PAIRS, 3, last=True)

            def mixture(ph):
                transpose_x(2 * ph * NCH)
                route(2 * ph * NCH, ph * NCH)
                transpose_comb(ph * NCH)
                pe.wait_ge(w_lo, 2 + 2 + 2 * GROUPS)
                with pe.Fori(0, NCH // 2 - 1) as cc:
                    chunk(ph, 2 * cc, 0, True)
                    chunk(ph, 2 * cc + 1, 1, True)
                chunk(ph, NCH - 2, 0, True)
                chunk(ph, NCH - 1, 1, False)

            def attention():
                pe.wait_ge(x_ready, NCH + 1)
                pe.wait_ge(att_loaded, 6 * 16)
                with pe.Fori(0, NCH) as b:
                    transpose_x(NCH + b)
                    pe.wait_ge(xT_ready, KH * (NCH + b + 1))
                    for j in range(TT):
                        if j < 2:
                            pe.wait_ge(x_mixed, b + 1)
                        else:
                            pe.wait_ge(z_ready, 2 * (TT * b + j - 1))
                        for k in range(KH):
                            i = nc.tensor.matmul(bank[j % 2][:, :], xT[:, k, j * P:(j + 1) * P],
                                                 w_att[:, k, 0:2 * H], start=(k == 0), stop=(k == KH - 1))
                        i.then_inc(proj_in_psum, 1)
                        for k in range(KH):
                            i = nc.tensor.matmul(bank[2 + j % 2][:, 0:H], xT[:, k, j * P:(j + 1) * P],
                                                 w_att[:, k, 2 * H:QVU], start=(k == 0), stop=(k == KH - 1))
                        i.then_inc(proj_in_psum, 1)
                    pe.wait_ge(kvu_ready, 2 * b + 1)
                    for k in range(KH):
                        for j in range(TT):
                            i = nc.tensor.transpose(tr_ps[k][:, j * P:(j + 1) * P],
                                                    z[:, j, k * P:(k + 1) * P], ident[:, :])
                    i.then_inc(kT_in_psum, 1)
                    pe.wait_ge(kvu_ready, 2 * b + 2)
                    for k in range(KH):
                        for j in range(TT):
                            i = nc.tensor.matmul(bank[0][:, k * P:(k + 1) * P], z[:, j, k * P:(k + 1) * P],
                                                 z[:, j, H + k * P:H + (k + 1) * P],
                                                 start=(j == 0), stop=(j == TT - 1))
                    i.then_inc(kv_in_psum, 1)
                    pe.wait_ge(qT_ready, KH * (b + 1))
                    pe.wait_ge(kv_ready, b + 1)
                    for j in range(TT):
                        for k in range(KH):
                            i = nc.tensor.matmul(y_ps[j // 2][:, (j % 2) * H + k * P:(j % 2) * H + (k + 1) * P],
                                                 qT[:, k, j * P:(j + 1) * P], kv[:, k, :],
                                                 start=True, stop=True)
                    i.then_inc(o_in_psum, 1)
                    pe.wait_ge(g_ready, b + 1)
                    for k in range(KH):
                        for j in range(TT):
                            i = nc.tensor.transpose(tr_ps[k][:, j * P:(j + 1) * P],
                                                    ez[:, j, k * P:(k + 1) * P], ident[:, :])
                    i.then_inc(gT_in_psum, 1)
                    pe.wait_ge(gT_ready, KH * (b + 1))
                    for j in range(TT):
                        for k in range(KH):
                            i = nc.tensor.matmul(y_ps[j // 2][:, (j % 2) * H:(j % 2 + 1) * H],
                                                 gT[:, k, j * P:(j + 1) * P], w_oa[:, k, :],
                                                 start=(k == 0), stop=(k == KH - 1))
                    i.then_inc(y_in_psum, 1)

            pe.wait_ge(consts, 3)
            pe.wait_ge(small_loaded, 48)
            mixture(0)
            attention()
            mixture(1)


_OUT_SHAPE = (8, 512, 256)


def kernel(**inputs):
    import numpy as np
    import concourse.bacc as bacc
    from concourse.bass_utils import run_bass_kernel_spmd as run

    a = {k: np.asarray(v) for k, v in inputs.items()}
    C, T, H = _OUT_SHAPE
    TT, KH = T // P, H // P
    E, I2, _ = a["L0_ffn_gate_up_proj"].shape
    I = I2 // 2

    def features_first(w):
        return w.reshape(w.shape[0], KH, P).transpose(2, 1, 0)

    laid = {
        "x": a["L0_attn_x"].reshape(C, P, TT, H),
        "gate_up": a["L0_ffn_gate_up_proj"].reshape(E // 2, 2, 2, I, KH, P).transpose(5, 0, 4, 2, 1, 3)
                   .reshape(P, E // 2, KH * 2 * P),
        "down": a["L0_ffn_down_proj"].reshape(E // 2, 2, H, I).transpose(1, 3, 0, 2).reshape(P, E // 2, H),
        "shared_gate_up": features_first(np.concatenate(
            [a["L0_ffn_shared_gate_w"], a["L0_ffn_shared_up_w"]])).reshape(P, KH * P),
        "shared_down": a["L0_ffn_shared_down_w"].T,
        "router": features_first(np.concatenate([a["L0_ffn_router_w"], a["L0_ffn_shared_expert_gate_w"]])),
        "w_qvu": np.concatenate([a["L0_attn_Wqk"], a["L0_attn_Wv"], a["L0_attn_Wu"]], axis=1)
                 .reshape(KH, P, 3 * H).transpose(1, 0, 2),
        "b_qvu": np.concatenate([a["L0_attn_bqk"], a["L0_attn_bv"], a["L0_attn_bu"]]),
        "w_o": a["L0_attn_Wo"].reshape(KH, P, H).transpose(1, 0, 2),
        "b_o": a["L0_attn_bo"],
        "ln_g": a["L0_attn_ln_g"],
        "ln_b": a["L0_attn_ln_b"],
    }
    nc = bacc.Bacc("TRN2", target_bir_lowering=False, num_devices=1)
    arrays, args = {}, []
    for name, v in laid.items():
        v = np.ascontiguousarray(v)
        arrays[f"in_{name}"] = v
        args.append(nc.dram_tensor(f"in_{name}", v.shape, mybir.dt.from_np(v.dtype), kind="ExternalInput").ap())
    args.append(nc.dram_tensor("result", (C, P, TT, H), F32, kind="ExternalOutput").ap())
    macaron_kernel(nc, *args)
    r = run(nc, [arrays], core_ids=[0])
    return r.results[0]["result"].reshape(_OUT_SHAPE)
```

```python
from contextlib import ExitStack

import concourse.bass as bass
from concourse import mybir

ALU = mybir.AluOpType
ACT = mybir.ActivationFunctionType
F32 = mybir.dt.float32
F16 = mybir.dt.float16
U32 = mybir.dt.uint32
AX_X = mybir.AxisListType.X
RMAX = bass.bass_isa.ReduceOp.max

P = 128


def macaron_kernel(nc, x_in, gate_up, down, shared_gate_up, shared_down, router,
                   w_qvu, b_qvu, w_o, b_o, ln_g, ln_b, out):
    NCH, _, TT, H = x_in.shape
    CH = P * TT
    KH = H // P
    PAIRS = gate_up.shape[1]
    E = 2 * PAIRS
    I = P // 2
    R = E + 1
    HD = 16
    QVU = 3 * H
    UNITS = PAIRS + 1
    TOPK = 8
    EPS = 1e-5
    LOWEST = -3.0e38

    GU = KH * 2 * P
    GROUP = 2
    SHIFT = 2 * GROUP
    GROUPS = PAIRS // GROUP
    LOADS = 4

    CW = 13
    COMB_SCALE = 2.0 ** (-4 - 2 * CW)

    ctx = ExitStack()
    with ctx:
        def sb(name, shape, dt):
            return ctx.enter_context(nc.sbuf_tensor(name, shape, dt))

        def sem(name):
            return ctx.enter_context(nc.semaphore(name))

        x = sb("x", [P, NCH * TT, H], F32)
        wgu = sb("wgu", [P, (PAIRS + SHIFT) * GU], F32)
        wd = sb("wd", [P, (PAIRS + SHIFT) * H], F32)
        wgu16 = wgu[:, :].bitcast(F16)
        wd16 = wd[:, :].bitcast(F16)
        ws_gu = sb("ws_gu", [P, 2 * KH * P], F16)
        ws_d = sb("ws_d", [P, 2 * H], F16)
        rw = sb("rw", [P, KH, R], F32)
        ident = sb("ident", [P, P], F32)
        head_mask = sb("head_mask", [P, P], F32)
        minus_half = sb("minus_half", [P, TT], F32)
        sc = sb("sc", [P, 8], F32)
        wmax = sb("wmax", [P, 16], F32)
        stats = sb("stats", [P, TT, 6], F32)
        mean_var = sb("mean_var", [P, TT, 2], F32)
        var_eps = sb("var_eps", [P, TT], F32)
        rstd = sb("rstd", [P, TT], F32)
        o_st = sb("o_st", [P, TT, 6], F32)
        o_mean_var = sb("o_mean_var", [P, TT, 2], F32)
        o_var_eps = sb("o_var_eps", [P, TT], F32)
        o_rs = sb("o_rs", [P, TT], F32)
        xn = sb("xn", [P, TT, H], F32)
        xT = sb("xT", [P, KH, CH], F32)
        xT_hi = sb("xT_hi", [P, 2, KH, CH], F16)
        xT_lo = sb("xT_lo", [P, 2, KH, CH], F16)
        logits = sb("logits", [P, TT, R], F32)
        top = sb("top", [P, TT, TOPK], F32)
        replaced = sb("replaced", [P, TT, E], F32)
        expo = sb("expo", [P, TT, E], F32)
        shared_th = sb("shared_th", [P, TT], F32)
        top_sum = sb("top_sum", [P, TT], F32)
        top_rec = sb("top_rec", [P, TT], F32)
        comb = sb("comb", [P, TT, R], F32)
        combT = sb("combT", [P, 2, CH], F32)
        kv = sb("kv", [P, KH, P], F32)

        SCRATCH = 16 * CH
        scratch = sb("scratch", [P, SCRATCH], F32)
        at = [0]

        def part(n):
            at[0] += n
            assert at[0] <= SCRATCH
            return scratch[:, at[0] - n:at[0]]

        cb = [part(CH) for _ in range(4)]
        cb_s = part(CH)
        th = [part(CH) for _ in range(2)]
        th_s = part(CH)
        act = [part(CH) for _ in range(2)]
        act_s = part(CH)
        act_hi = [part(CH // 2).bitcast(F16) for _ in range(4)]
        act_lo = [part(CH // 2).bitcast(F16) for _ in range(4)]
        act_hi_s = part(CH // 2).bitcast(F16)
        act_lo_s = part(CH // 2).bitcast(F16)
        at[0] = 0
        z = part(TT * QVU).rearrange("p (j n) -> p j n", j=TT)
        ez = part(TT * QVU).rearrange("p (j n) -> p j n", j=TT)
        u_gate = part(TT * H).rearrange("p (j n) -> p j n", j=TT)
        o = part(TT * H).rearrange("p (j n) -> p j n", j=TT)
        qT = xT_hi[:, :, :, :].rearrange("p a k n -> p (a k n)").bitcast(F32).rearrange(
            "p (k n) -> p k n", k=KH)
        gT = xT_lo[:, :, :, :].rearrange("p a k n -> p (a k n)").bitcast(F32).rearrange(
            "p (k n) -> p k n", k=KH)
        s_gu32 = scratch[:, 0:KH * P]
        s_d32 = scratch[:, KH * P:KH * P + H]
        w_att = wgu[:, PAIRS * GU:PAIRS * GU + KH * QVU].rearrange("p (k n) -> p k n", k=KH)
        w_oa = wgu[:, PAIRS * GU + KH * QVU:PAIRS * GU + KH * QVU + KH * H].rearrange(
            "p (k n) -> p k n", k=KH)
        assert SHIFT * GU >= KH * (QVU + H) and SHIFT * H >= H
        b_att = sb("b_att", [P, QVU], F32)
        g_row = wd[:, PAIRS * H:PAIRS * H + H]
        b_row = wd[:, PAIRS * H + H:PAIRS * H + 2 * H]
        bo_row = wd[:, PAIRS * H + 2 * H:PAIRS * H + 3 * H]

        combT_dram = nc.dram_tensor("combT_dram", (2, R, CH), F32, kind="Internal").ap()

        LN_ATT = NCH

        def attention_steps(engine, first, step, last):
            first()
            step(0, False, True, True)
            with engine.Fori(1, NCH - 2) as i:
                step(i, True, True, True)
            step(NCH - 2, True, True, False)
            step(NCH - 1, True, False, False)
            last()

        bank = [ctx.enter_context(nc.psum_tensor(f"bank{i}", [P, 512], F32)) for i in range(8)]
        gate_ps, up_ps, y_ps = bank[0:2], bank[2:4], bank[4:6]
        tr_ps = bank[6:8]
        shared_ps, router_ps, comb_ps = bank[6], bank[6], bank[7]

        x_loaded = sem("x_loaded")
        w_loaded = [sem(f"w_loaded{i}") for i in range(LOADS)]
        small_loaded = sem("small_loaded")
        att_loaded = sem("att_loaded")
        waits_apart = sem("waits_apart")
        consts = sem("consts")
        const_step = sem("const_step")
        wmax_parts = sem("wmax_parts")
        wmax_rows = sem("wmax_rows")
        wmax_all = sem("wmax_all")
        scale_step = sem("scale_step")
        scales_ready = sem("scales_ready")
        w_hi = sem("w_hi")
        w_lo = sem("w_lo")
        bn_done = sem("bn_done")
        stats_ready = sem("stats_ready")
        var_ready = sem("var_ready")
        rstd_ready = sem("rstd_ready")
        xn_ready = sem("xn_ready")
        xT_in_psum = sem("xT_in_psum")
        xT_ready = sem("xT_ready")
        xhi_ready = sem("xhi_ready")
        xlo_ready = sem("xlo_ready")
        router_in_psum = sem("router_in_psum")
        logits_ready = sem("logits_ready")
        top_done = sem("top_done")
        replaced_done = sem("replaced_done")
        shifted_ready = sem("shifted_ready")
        exp_ready = sem("exp_ready")
        comb_step = sem("comb_step")
        comb_ready = sem("comb_ready")
        comb_in_psum = sem("comb_in_psum")
        combT_ready = sem("combT_ready")
        combT_stored = sem("combT_stored")
        cb_loaded = [sem(f"cb_loaded{i}") for i in range(4)]
        cbs_loaded = sem("cbs_loaded")
        gu_ready = sem("gu_ready")
        th_ready = sem("th_ready")
        gated = sem("gated")
        prod_ready = sem("prod_ready")
        act_ready = sem("act_ready")
        hi_ready = sem("hi_ready")
        lo_ready = sem("lo_ready")
        down_done = sem("down_done")
        x_ready = sem("x_ready")
        out_stored = sem("out_stored")
        proj_in_psum = sem("proj_in_psum")
        z_ready = sem("z_ready")
        ez_ready = sem("ez_ready")
        em_ready = sem("em_ready")
        kv_rows_ready = sem("kv_rows_ready")
        u_ready = sem("u_ready")
        kv_in_psum = sem("kv_in_psum")
        kv_ready = sem("kv_ready")
        kT_in_psum = sem("kT_in_psum")
        qT_ready = sem("qT_ready")
        o_in_psum = sem("o_in_psum")
        o_ready = sem("o_ready")
        o_bn = sem("o_bn")
        o_stats = sem("o_stats")
        o_var = sem("o_var")
        o_rstd = sem("o_rstd")
        o_gained = sem("o_gained")
        o_normed = sem("o_normed")
        g_ready = sem("g_ready")
        gT_in_psum = sem("gT_in_psum")
        gT_ready = sem("gT_ready")
        xb_ready = sem("xb_ready")
        y_in_psum = sem("y_in_psum")
        x_mixed = sem("x_mixed")

        PRIME = 4

        def unit(ph, c, u):
            return PRIME + ph * NCH * UNITS + c * UNITS + u

        SHARED = 0

        PASSES = ((0, 0), (0, 1), (1, 0))

        def tiles(c):
            return x[:, bass.ds(c * TT, TT), :]

        def tile_of(c, j):
            return x[:, bass.ds(c * TT + j, 1), :].rearrange("p a n -> p (a n)")


        def gu32(g):
            return wgu[:, bass.ds((g * GROUP + SHIFT) * GU, GROUP * GU)].rearrange(
                "p (a n) -> p a n", a=GROUP)

        def d32(g):
            return wd[:, bass.ds((g * GROUP + SHIFT) * H, GROUP * H)].rearrange(
                "p (a n) -> p a n", a=GROUP)

        def gu_half(g, part_):
            return wgu16[:, bass.ds(g * GROUP * 2 * GU, GROUP * 2 * GU)].rearrange(
                "p (a s n) -> p a s n", a=GROUP, s=2)[:, :, part_, :]

        def d_half(g, part_):
            return wd16[:, bass.ds(g * GROUP * 2 * H, GROUP * 2 * H)].rearrange(
                "p (a s n) -> p a s n", a=GROUP, s=2)[:, :, part_, :]

        def apart(engine):
            engine.sem_inc(waits_apart, 1)

        block = ctx.enter_context(nc.Block())

        @block.sync
        def _(sp):
            sp.dma_start(x[:, :, :].rearrange("p (c j) h -> p c (j h)", c=NCH),
                         x_in.rearrange("c p j h -> p c (j h)")).then_inc(x_loaded, 16)
            sp.dma_start(rw[:, :, :], router).then_inc(small_loaded, 16)
            sp.dma_start(s_gu32, shared_gate_up).then_inc(small_loaded, 16)
            sp.dma_start(s_d32[64:128, :], shared_down).then_inc(small_loaded, 16)
            n = PAIRS // LOADS
            for i in range(LOADS):
                sp.dma_start(wgu[:, (SHIFT + i * n) * GU:(SHIFT + (i + 1) * n) * GU],
                             gate_up[:, i * n:(i + 1) * n, :].rearrange("p a n -> p (a n)")
                             ).then_inc(w_loaded[i], 16)
                sp.dma_start(wd[:, (SHIFT + i * n) * H:(SHIFT + (i + 1) * n) * H],
                             down[:, i * n:(i + 1) * n, :].rearrange("p a n -> p (a n)")
                             ).then_inc(w_loaded[i], 16)

            sp.wait_ge(w_lo, 2 + 2 * GROUPS + 2)
            sp.dma_start(w_att, w_qvu).then_inc(att_loaded, 16)
            sp.dma_start(w_oa, w_o).then_inc(att_loaded, 16)
            sp.dma_start(b_att[:, :], b_qvu.partition_broadcast(P)).then_inc(att_loaded, 16)
            for row, vec in ((g_row, ln_g), (b_row, ln_b), (bo_row, b_o)):
                sp.dma_start(row, vec.partition_broadcast(P)).then_inc(att_loaded, 16)

            def spread(dst, par, row, done):
                src = combT_dram[par, bass.ds(row, 1), :].rearrange("a n -> (a n)")
                sp.dma_start(dst, src.partition_broadcast(I)).then_inc(done, 16)

            def pair(ph, c, u, par, i):
                sp.wait_ge(act_ready, unit(ph, c, u) - 3)
                spread(cb[i][0:I, :], par, 2 * (u - 1), cb_loaded[i])
                spread(cb[i][I:P, :], par, 2 * (u - 1) + 1, cb_loaded[i])

            def chunk(ph, c, par, store_last=False):
                sp.wait_ge(combT_ready, ph * NCH + c + 1)
                sp.dma_start(combT_dram[par, :, :], combT[0:R, par, :]).then_inc(combT_stored, 16)
                sp.wait_ge(combT_stored, 16 * (ph * NCH + c + 1))
                spread(cb_s[I:P, :], par, E, cbs_loaded)
                for i in range(4):
                    pair(ph, c, i + 1, par, i)
                if store_last:
                    store(c - 1)
                with sp.Fori(1, PAIRS // 4) as q:
                    for i in range(4):
                        pair(ph, c, 4 * q + i + 1, par, i)

            def store(c):
                sp.wait_ge(x_ready, NCH + c + 2)
                sp.dma_start(out[bass.ds(c, 1), :, :, :].rearrange("a p j h -> p (a j h)"),
                             tiles(c).rearrange("p j h -> p (j h)")).then_inc(out_stored, 16)

            with sp.Fori(0, NCH // 2) as cc:
                chunk(0, 2 * cc, 0)
                chunk(0, 2 * cc + 1, 1)
            chunk(1, 0, 0)
            chunk(1, 1, 1, True)
            with sp.Fori(1, NCH // 2) as cc:
                chunk(1, 2 * cc, 0, True)
                chunk(1, 2 * cc + 1, 1, True)
            store(NCH - 1)
            sp.wait_ge(out_stored, 16 * NCH)

        @block.gpsimd
        def _(pool):
            nc.gpsimd.memset(ident[:, :], 0.0).then_inc(const_step, 1)
            nc.gpsimd.memset(head_mask[:, :], 0.5).then_inc(const_step, 1)
            nc.gpsimd.memset(minus_half[:, :], -0.5).then_inc(consts, 1)
            pool.wait_ge(const_step, 2)
            nc.gpsimd.affine_select(out=ident[:, :], in_=ident[:, :], compare_op=ALU.not_equal, fill=1.0,
                                    base=0, pattern=[[-1, P]], channel_multiplier=1).then_inc(consts, 1)
            heads = head_mask[:, :].rearrange("p (a d) -> p a d", d=HD)
            nc.gpsimd.affine_select(out=heads, in_=heads, compare_op=ALU.is_ge, fill=0.0, base=0,
                                    pattern=[[-HD, P // HD], [0, HD]], channel_multiplier=1
                                    ).then_inc(const_step, 1)
            pool.wait_ge(const_step, 3)
            nc.gpsimd.affine_select(out=heads, in_=heads, compare_op=ALU.is_ge, fill=0.0, base=HD - 1,
                                    pattern=[[HD, P // HD], [0, HD]], channel_multiplier=-1
                                    ).then_inc(consts, 1)
            pool.sem_inc(act_ready, PRIME)

            def ln_rstd(n):
                pool.wait_ge(stats_ready, TT * (n + 1))
                apart(pool)
                nc.gpsimd.tensor_scalar(var_eps[:, :], mean_var[:, :, 1], EPS, None, ALU.add
                                        ).then_inc(var_ready, 1)
                pool.wait_ge(var_ready, n + 1)
                nc.gpsimd.tensor_tensor(rstd[:, :], var_eps[:, :], minus_half[:, :], ALU.pow
                                        ).then_inc(rstd_ready, 1)

            def weigh(w, buf, weights):
                pool.wait_ge(prod_ready, w + 1)
                nc.gpsimd.tensor_tensor(buf, buf, weights, ALU.mult).then_inc(act_ready, 1)

            def pair(ph, c, u, q, i):
                pool.wait_ge(cb_loaded[i], 32 * ((ph * NCH + c) * (PAIRS // 4) + q + 1))
                weigh(unit(ph, c, u), act[i % 2], cb[i])

            def pairs_of(ph, c, q):
                for i in range(4):
                    pair(ph, c, 4 * q + 3 + i, q + (2 + i) // 4, (2 + i) % 4)

            def pairs(ph, c, q0, q1):
                with pool.Fori(q0, q1) as q:
                    pairs_of(ph, c, q)

            def chunk(ph, c, par, nxt):
                pool.wait_ge(cbs_loaded, 16 * (ph * NCH + c + 1))
                pool.wait_ge(act_ready, unit(ph, c, SHARED))
                weigh(unit(ph, c, SHARED), act_s[I:P, :], cb_s[I:P, :])
                pool.wait_ge(act_ready, unit(ph, c, SHARED) + 1)
                pair(ph, c, 1, 0, 0)
                if nxt or ph == 0:
                    ln_rstd(2 * ph * NCH + c + 1)
                pair(ph, c, 2, 0, 1)
                pairs(ph, c, 0, 2)
                pairs(ph, c, 2, 4)
                if not nxt and ph == 0:
                    ln_rstd(LN_ATT + 1)
                pairs(ph, c, 4, 6)
                pairs_of(ph, c, 6)
                pair(ph, c, PAIRS - 1, PAIRS // 4 - 1, 2)
                pair(ph, c, PAIRS, PAIRS // 4 - 1, 3)

            def mixture(ph):
                if ph == 0:
                    ln_rstd(0)
                    pool.wait_ge(wmax_rows, 2)
                    nc.gpsimd.partition_all_reduce(wmax[:, 14:16], wmax[:, 12:14], P, RMAX
                                                   ).then_inc(wmax_all, 1)
                with pool.Fori(0, NCH // 2 - 1) as cc:
                    chunk(ph, 2 * cc, 0, True)
                    chunk(ph, 2 * cc + 1, 1, True)
                chunk(ph, NCH - 2, 0, True)
                chunk(ph, NCH - 1, 1, False)

            def attention():
                def elu_low(b, j):
                    pool.wait_ge(ez_ready, 2 * (TT * b + j) + 1)
                    apart(pool)
                    nc.gpsimd.tensor_scalar(ez[:, j, 0:H], ez[:, j, 0:H], 1.0, -1.0, ALU.min, ALU.add
                                            ).then_inc(em_ready, 1)

                def out_rstd(b):
                    pool.wait_ge(o_stats, TT * (b + 1))
                    apart(pool)
                    nc.gpsimd.tensor_scalar(o_var_eps[:, :], o_mean_var[:, :, 1], EPS, None, ALU.add
                                            ).then_inc(o_var, 1)
                    pool.wait_ge(o_var, b + 1)
                    nc.gpsimd.tensor_tensor(o_rs[:, :], o_var_eps[:, :], minus_half[:, :], ALU.pow
                                            ).then_inc(o_rstd, 1)

                def add_bo(b):
                    pool.wait_ge(xn_ready, LN_ATT + b + 1)
                    nc.gpsimd.tensor_tensor(tiles(b), tiles(b),
                                            bo_row[:, None, :].broadcast_to([P, TT, H]), ALU.add
                                            ).then_inc(xb_ready, 1)

                def out_gate(b):
                    for j in range(TT):
                        pool.wait_ge(o_normed, TT * b + j + 1)
                        nc.gpsimd.tensor_tensor(o[:, j, :], o[:, j, :], u_gate[:, j, :], ALU.mult
                                                ).then_inc(g_ready, 1)

                def first():
                    pool.wait_ge(att_loaded, 6 * 16)
                    for j in range(TT - 1):
                        elu_low(0, j)

                def step(i, prev, nxt, after):
                    elu_low(i, TT - 1)
                    if prev:
                        add_bo(i - 1)
                    if nxt:
                        ln_rstd(LN_ATT + i + 2)
                    if nxt:
                        elu_low(i + 1, 0)
                    out_rstd(i)
                    if nxt:
                        elu_low(i + 1, 1)
                    out_gate(i)
                    if nxt:
                        elu_low(i + 1, 2)

                attention_steps(pool, first, step, lambda: add_bo(NCH - 1))

            mixture(0)
            attention()
            mixture(1)

        @block.scalar
        def _(act_e):
            act_e.sem_inc(th_ready, PRIME)
            act_e.sem_inc(hi_ready, PRIME)
            act_e.sem_inc(w_hi, 2)

            def split_hi(n, out, in_, scale):
                act_e.wait_ge(w_lo, n)
                nc.scalar.activation(out, in_, ACT.Copy, scale=scale).then_inc(w_hi, 1)

            def xT_out(n, m, par, hi_too=True):
                act_e.wait_ge(xT_in_psum, KH * (n + 1))
                if not (isinstance(m, int) and m == 0):
                    act_e.wait_ge(router_in_psum, m)
                for k in range(KH):
                    nc.scalar.activation(xT[:, k, :], tr_ps[k][:, :], ACT.Copy).then_inc(xT_ready, 1)
                if hi_too:
                    for k in range(KH):
                        nc.scalar.activation(xT_hi[:, par, k, :], tr_ps[k][:, :], ACT.Copy
                                             ).then_inc(xhi_ready, 1)

            def logits_out(m, ps=router_ps):
                act_e.wait_ge(router_in_psum, m + 1)
                nc.scalar.activation(logits[:, :, :].rearrange("p j n -> p (j n)"),
                                     ps[:, 0:TT * R], ACT.Copy).then_inc(logits_ready, 1)

            def router_exp(m):
                act_e.wait_ge(shifted_ready, m + 1)
                nc.scalar.activation(expo[:, :, :], expo[:, :, :], ACT.Exp).then_inc(exp_ready, 1)
                nc.scalar.activation(shared_th[:, :], logits[:, :, E], ACT.Tanh, scale=0.5
                                     ).then_inc(exp_ready, 1)

            def comb_out(m, par, ps=comb_ps):
                act_e.wait_ge(comb_in_psum, m + 1)
                nc.scalar.activation(combT[0:R, par, :], ps[0:R, :], ACT.Copy, scale=COMB_SCALE
                                     ).then_inc(combT_ready, 1)

            def tanh(w, out, ps):
                act_e.wait_ge(gu_ready, 2 * w + 1)
                act_e.wait_ge(gated, w - 1)
                nc.scalar.activation(out, ps, ACT.Tanh, scale=sc[0:out.shape[0], 4:5]).then_inc(th_ready, 1)

            def hi(w, out, buf):
                act_e.wait_ge(act_ready, w + 1)
                act_e.wait_ge(down_done, w - 3)
                nc.scalar.activation(out, buf, ACT.Copy).then_inc(hi_ready, 1)

            def pair(ph, c, u, i, before):
                tanh(unit(ph, c, u), th[i % 2], gate_ps[i % 2][:, :])
                hi(unit(ph, c, u) - 1, act_hi[before], act[before % 2])

            def pairs_of(ph, c, q):
                for i in range(4):
                    pair(ph, c, 4 * q + 3 + i, (2 + i) % 4, (1 + i) % 4)

            def pairs(ph, c, q0, q1):
                with act_e.Fori(q0, q1) as q:
                    pairs_of(ph, c, q)

            def chunk(ph, c, par, nxt):
                n, m = 2 * ph * NCH + c + 1, ph * NCH + c + 1
                tanh(unit(ph, c, SHARED), th_s[0:I, :], shared_ps[0:I, :])
                hi(unit(ph, c, SHARED), act_hi_s[I:P, :], act_s[I:P, :])
                tanh(unit(ph, c, 1), th[0], gate_ps[0][:, :])
                pair(ph, c, 2, 1, 0)
                pairs(ph, c, 0, 2)
                if nxt or ph == 0:
                    xT_out(n, m, 1 - par, nxt)
                pairs(ph, c, 2, 4)
                if nxt:
                    logits_out(m)
                pairs(ph, c, 4, 6)
                if nxt:
                    router_exp(m)
                pairs_of(ph, c, 6)
                if nxt:
                    comb_out(m, 1 - par)
                pair(ph, c, PAIRS - 1, 2, 1)
                pair(ph, c, PAIRS, 3, 2)
                hi(unit(ph, c, PAIRS), act_hi[3], act[1])

            def mixture(ph):
                if ph == 0:
                    xT_out(0, 0, 0)
                    logits_out(0)
                    router_exp(0)
                    comb_out(0, 0)
                    act_e.wait_ge(scales_ready, 1)
                    split_hi(2, ws_gu[:, 0:KH * P], s_gu32, sc[:, 2:3])
                    split_hi(2, ws_d[I:P, 0:H], s_d32[I:P, :], sc[I:P, 3:4])
                    with act_e.Fori(0, GROUPS) as g:
                        split_hi(2 * g + 2, gu_half(g, 0), gu32(g), sc[:, 2:3])
                        split_hi(2 * g + 3, d_half(g, 0), d32(g), sc[:, 3:4])
                with act_e.Fori(0, NCH // 2 - 1) as cc:
                    chunk(ph, 2 * cc, 0, True)
                    chunk(ph, 2 * cc + 1, 1, True)
                chunk(ph, NCH - 2, 0, True)
                chunk(ph, NCH - 1, 1, False)

            def attention():
                def copy_out(ready, b, src, dst, done, scale=1.0):
                    for k in range(KH):
                        act_e.wait_ge(ready, KH * b + k + 1)
                        nc.scalar.activation(dst(k), src[k][:, :], ACT.Copy, scale=scale).then_inc(done, 1)

                def exp_tanh(b, j):
                    act_e.wait_ge(z_ready, 2 * (TT * b + j) + 1)
                    nc.scalar.activation(ez[:, j, 0:H], z[:, j, 0:H], ACT.Exp).then_inc(ez_ready, 1)
                    act_e.wait_ge(z_ready, 2 * (TT * b + j) + 2)
                    nc.scalar.activation(ez[:, j, H:QVU], z[:, j, H:QVU], ACT.Tanh, scale=0.5
                                         ).then_inc(ez_ready, 1)

                def xT_copy(b):
                    copy_out(xT_in_psum, LN_ATT + b, y_ps, lambda k: xT[:, k, :], xT_ready)

                def gT_copy(b):
                    copy_out(gT_in_psum, b, tr_ps, lambda k: gT[:, k, :], gT_ready, scale=0.5)

                def first():
                    for j in range(TT - 1):
                        exp_tanh(0, j)

                def step(i, prev, nxt, after):
                    xT_copy(i + 1)
                    if prev:
                        gT_copy(i - 1)
                    exp_tanh(i, TT - 1)
                    copy_out(kT_in_psum, i, y_ps, lambda k: qT[:, k, :], qT_ready)
                    copy_out(o_in_psum, i, y_ps,
                             lambda h: o[:, 2 * h:2 * h + 2, :].rearrange("p j n -> p (j n)"), o_ready)
                    if nxt:
                        exp_tanh(i + 1, 0)
                        exp_tanh(i + 1, 1)
                        exp_tanh(i + 1, 2)

                def last():
                    logits_out(NCH, bank[0])
                    for k in range(KH):
                        nc.scalar.activation(xT_hi[:, 0, k, :], xT[:, k, :], ACT.Copy
                                             ).then_inc(xhi_ready, 1)
                    router_exp(NCH)
                    gT_copy(NCH - 1)
                    comb_out(NCH, 0, bank[1])

                attention_steps(act_e, first, step, last)

            mixture(0)
            attention()
            mixture(1)

        @block.vector
        def _(dve):
            for s in (gated, prod_ready, lo_ready):
                dve.sem_inc(s, PRIME)
            dve.sem_inc(x_ready, 1)
            dve.sem_inc(x_mixed, 1)
            dve.sem_inc(w_lo, 2)

            def ln_stats(n, c, updated, count):
                dve.wait_ge(updated, count)
                for j in range(TT):
                    nc.vector.bn_stats(stats[:, j, :], tile_of(c, j)).then_inc(bn_done, 1)
                dve.wait_ge(bn_done, TT * (n + 1))
                apart(dve)
                for j in range(TT):
                    nc.vector.bn_aggr(mean_var[:, j, :], stats[:, j, :]).then_inc(stats_ready, 1)

            def ln_apply(n, c):
                dve.wait_ge(rstd_ready, n + 1)
                for j in range(TT):
                    i = nc.vector.tensor_scalar(xn[:, j, :], tile_of(c, j), mean_var[:, j, 0:1],
                                                rstd[:, j:j + 1], ALU.subtract, ALU.mult)
                i.then_inc(xn_ready, 1)

            def xT_low(m, par):
                dve.wait_ge(xhi_ready, KH * (m + 1))
                for k in range(KH):
                    nc.vector.tensor_tensor(xT_lo[:, par, k, :], tr_ps[k][:, :], xT_hi[:, par, k, :],
                                            ALU.subtract).then_inc(xlo_ready, 1)

            def router_top(m):
                dve.wait_ge(logits_ready, m + 1)
                apart(dve)
                for j in range(TT):
                    nc.vector.max(top[:, j, :], logits[:, j, 0:E]).then_inc(top_done, 1)
                dve.wait_ge(top_done, TT * (m + 1))
                apart(dve)
                for j in range(TT):
                    nc.vector.match_replace(replaced[:, j, :], top[:, j, :], logits[:, j, 0:E], LOWEST
                                            ).then_inc(replaced_done, 1)
                nc.vector.tensor_tensor(expo[:, :, :], logits[:, :, 0:E],
                                        top[:, :, 0:1].broadcast_to([P, TT, E]), ALU.subtract
                                        ).then_inc(shifted_ready, 1)
                dve.wait_ge(replaced_done, TT * (m + 1))
                nc.vector.tensor_tensor(replaced[:, :, :], logits[:, :, 0:E], replaced[:, :, :],
                                        ALU.not_equal).then_inc(comb_step, 1)

            def router_weights(m):
                dve.wait_ge(exp_ready, 2 * (m + 1))
                dve.wait_ge(comb_step, 4 * m + 1)
                nc.vector.tensor_tensor(expo[:, :, :], expo[:, :, :], replaced[:, :, :], ALU.mult
                                        ).then_inc(comb_step, 1)
                dve.wait_ge(comb_step, 4 * m + 2)
                nc.vector.reduce_sum(top_sum[:, :], expo[:, :, :], AX_X).then_inc(comb_step, 1)
                dve.wait_ge(comb_step, 4 * m + 3)
                nc.vector.reciprocal(top_rec[:, :], top_sum[:, :]).then_inc(comb_step, 1)
                nc.vector.tensor_scalar(comb[:, :, E], shared_th[:, :], 0.5, 0.5, ALU.mult, ALU.add
                                        ).then_inc(comb_ready, 1)
                dve.wait_ge(comb_step, 4 * m + 4)
                nc.vector.tensor_tensor(comb[:, :, 0:E], expo[:, :, :],
                                        top_rec[:, :, None].broadcast_to([P, TT, E]), ALU.mult
                                        ).then_inc(comb_ready, 1)

            def gate(w, buf, gate_in, up_in, th_in, buf_up=None):
                dve.wait_ge(lo_ready, w - 1)
                dve.wait_ge(th_ready, w + 1)
                nc.vector.scalar_tensor_tensor(out=buf, in0=th_in, scalar=1.0, in1=gate_in,
                                               op0=ALU.add, op1=ALU.mult).then_inc(gated, 1)
                dve.wait_ge(gu_ready, 2 * w + 2)
                dve.wait_ge(gated, w + 1)
                nc.vector.tensor_tensor(buf, buf, up_in, ALU.mult).then_inc(prod_ready, 1)

            def low(w, out, buf, hi_in):
                dve.wait_ge(hi_ready, w + 1)
                nc.vector.tensor_tensor(out, buf, hi_in, ALU.subtract).then_inc(lo_ready, 1)

            def low_s(w):
                low(w, act_lo_s[I:P, :], act_s[I:P, :], act_hi_s[I:P, :])

            def gate_s(w):
                gate(w, act_s[I:P, :], shared_ps[0:I, :], shared_ps[I:P, :], th_s[0:I, :])

            def gate_pair(w, i):
                gate(w, act[i % 2], gate_ps[i % 2][:, :], up_ps[i % 2][:, :], th[i % 2])

            def pair(ph, c, u, i, before):
                gate_pair(unit(ph, c, u), i)
                low(unit(ph, c, u) - 1, act_lo[before], act[before % 2], act_hi[before])

            def pairs_of(ph, c, q):
                for i in range(4):
                    pair(ph, c, 4 * q + 3 + i, (2 + i) % 4, (1 + i) % 4)

            def pairs(ph, c, q0, q1):
                with dve.Fori(q0, q1) as q:
                    pairs_of(ph, c, q)

            def chunk(ph, c, par, nxt):
                n, m = 2 * ph * NCH + c + 1, ph * NCH + c + 1
                low_s(unit(ph, c, SHARED))
                gate_pair(unit(ph, c, 1), 0)
                if ph == 0 and not nxt:
                    ln_stats(LN_ATT, 0, x_ready, 2)
                elif ph == 0:
                    ln_stats(n, c + 1, x_loaded, 16)
                elif nxt:
                    ln_stats(n, c + 1, x_mixed, NCH + 1)
                pair(ph, c, 2, 1, 0)
                if nxt:
                    ln_apply(n, c + 1)
                elif ph == 0:
                    ln_apply(LN_ATT, 0)
                pairs(ph, c, 0, 2)
                if nxt:
                    xT_low(m, 1 - par)
                elif ph == 0:
                    ln_stats(LN_ATT + 1, 1, x_ready, 3)
                pairs(ph, c, 2, 4)
                if nxt:
                    router_top(m)
                elif ph == 0:
                    dve.wait_ge(xT_in_psum, KH * (LN_ATT + 1))
                    ln_apply(LN_ATT + 1, 1)
                pairs(ph, c, 4, 6)
                if nxt:
                    router_weights(m)
                pairs_of(ph, c, 6)
                pair(ph, c, PAIRS - 1, 2, 1)
                pair(ph, c, PAIRS, 3, 2)
                low(unit(ph, c, PAIRS), act_lo[3], act[1], act_hi[3])
                if nxt:
                    gate_s(unit(ph, c + 1, SHARED))
                dve.wait_ge(down_done, unit(ph, c, PAIRS) + 1)
                for h in range(2):
                    rows = x[:, bass.ds(c * TT + 2 * h, 2), :].rearrange("p a n -> p (a n)")
                    i = nc.vector.scalar_tensor_tensor(out=rows, in0=y_ps[h][:, :], scalar=sc[:, 5:6],
                                                       in1=rows, op0=ALU.mult, op1=ALU.add)
                i.then_inc(x_ready, 1)

            def ready_first():
                ln_stats(0, 0, x_loaded, 16)
                ln_apply(0, 0)
                xT_low(0, 0)
                router_top(0)
                router_weights(0)

            def split_lo(n, out, in_, scale, hi_in):
                dve.wait_ge(w_hi, n + 1)
                nc.vector.scalar_tensor_tensor(out=out, in0=in_, scalar=scale, in1=hi_in,
                                               op0=ALU.mult, op1=ALU.subtract).then_inc(w_lo, 1)

            def weight_scales():
                dve.wait_ge(small_loaded, 48)
                nc.vector.memset(wmax[:, 9:12], 0.0).then_inc(wmax_parts, 1)
                dve.wait_ge(wmax_parts, 1)
                nc.vector.tensor_reduce(wmax[:, 4:5], s_gu32, AX_X, ALU.max, apply_absolute_value=True
                                        ).then_inc(wmax_parts, 1)
                nc.vector.tensor_reduce(wmax[I:P, 9:10], s_d32[I:P, :], AX_X, ALU.max,
                                        apply_absolute_value=True).then_inc(wmax_parts, 1)
                n = PAIRS // LOADS
                for i in range(LOADS):
                    dve.wait_ge(w_loaded[i], 32)
                    nc.vector.tensor_reduce(wmax[:, i:i + 1],
                                            wgu[:, (SHIFT + i * n) * GU:(SHIFT + (i + 1) * n) * GU],
                                            AX_X, ALU.max, apply_absolute_value=True).then_inc(wmax_parts, 1)
                    nc.vector.tensor_reduce(wmax[:, 5 + i:6 + i],
                                            wd[:, (SHIFT + i * n) * H:(SHIFT + (i + 1) * n) * H],
                                            AX_X, ALU.max, apply_absolute_value=True).then_inc(wmax_parts, 1)
                dve.wait_ge(wmax_parts, 3 + 2 * LOADS)
                nc.vector.tensor_reduce(wmax[:, 12:13], wmax[:, 0:5], AX_X, ALU.max).then_inc(wmax_rows, 1)
                nc.vector.tensor_reduce(wmax[:, 13:14], wmax[:, 5:10], AX_X, ALU.max).then_inc(wmax_rows, 1)
                dve.wait_ge(wmax_all, 1)
                bits = sc[:, :].bitcast(U32)
                nc.vector.tensor_scalar(bits[:, 0:2], wmax[:, 14:16].bitcast(U32), 0x7F800000, None,
                                        ALU.bitwise_and).then_inc(scale_step, 1)
                dve.wait_ge(scale_step, 1)
                nc.vector.tensor_scalar(sc[:, 0:2], sc[:, 0:2], 2.0 ** -63, None, ALU.max
                                        ).then_inc(scale_step, 1)
                dve.wait_ge(scale_step, 2)
                nc.vector.tensor_scalar(bits[:, 2:4], bits[:, 0:2], -1.0, float((254 + CW) << 23),
                                        ALU.mult, ALU.add).then_inc(scale_step, 1)
                nc.vector.tensor_scalar(sc[:, 4:5], sc[:, 0:1], 2.0 ** (-CW - 1), None, ALU.mult
                                        ).then_inc(scale_step, 1)
                nc.vector.tensor_scalar(sc[:, 6:7], sc[:, 0:1], sc[:, 0:1], 2.0 ** (2 - CW),
                                        ALU.mult, ALU.mult).then_inc(scale_step, 1)
                dve.wait_ge(scale_step, 5)
                nc.vector.tensor_scalar(sc[:, 5:6], sc[:, 6:7], sc[:, 1:2], None, ALU.mult
                                        ).then_inc(scale_step, 1)
                dve.wait_ge(scale_step, 6)
                dve.sem_inc(scales_ready, 1)
                split_lo(2, ws_gu[:, KH * P:2 * KH * P], s_gu32, sc[:, 2:3], ws_gu[:, 0:KH * P])
                split_lo(3, ws_d[I:P, H:2 * H], s_d32[I:P, :], sc[I:P, 3:4], ws_d[I:P, 0:H])
                with dve.Fori(0, GROUPS) as g:
                    split_lo(2 * g + 4, gu_half(g, 1), gu32(g), sc[:, 2:3], gu_half(g, 0))
                    split_lo(2 * g + 5, d_half(g, 1), d32(g), sc[:, 3:4], d_half(g, 0))

            def mixture(ph):
                if ph == 0:
                    ready_first()
                    weight_scales()
                gate_s(unit(ph, 0, SHARED))
                with dve.Fori(0, NCH // 2 - 1) as cc:
                    chunk(ph, 2 * cc, 0, True)
                    chunk(ph, 2 * cc + 1, 1, True)
                chunk(ph, NCH - 2, 0, True)
                chunk(ph, NCH - 1, 1, False)

            def attention():
                def add_bias_kv(b, j):
                    dve.wait_ge(proj_in_psum, 2 * (TT * b + j) + 1)
                    nc.vector.tensor_tensor(z[:, j, 0:2 * H], bank[j % 2][:, :], b_att[:, 0:2 * H],
                                            ALU.add).then_inc(z_ready, 1)

                def add_bias_u(b, j):
                    dve.wait_ge(proj_in_psum, 2 * (TT * b + j) + 2)
                    nc.vector.tensor_tensor(z[:, j, 2 * H:QVU], bank[2 + j % 2][:, 0:H],
                                            b_att[:, 2 * H:QVU], ALU.add).then_inc(z_ready, 1)

                def add_bias(b, j):
                    add_bias_kv(b, j)
                    add_bias_u(b, j)

                def kv_rows(b, j):
                    dve.wait_ge(em_ready, TT * b + j + 1)
                    nc.vector.scalar_tensor_tensor(out=z[:, j, 0:H], in0=z[:, j, 0:H], scalar=0.0,
                                                   in1=ez[:, j, 0:H], op0=ALU.max, op1=ALU.add
                                                   ).then_inc(kv_rows_ready, 1)
                    dve.wait_ge(ez_ready, 2 * (TT * b + j) + 2)
                    nc.vector.scalar_tensor_tensor(out=z[:, j, H:2 * H], in0=ez[:, j, H:2 * H], scalar=1.0,
                                                   in1=z[:, j, H:2 * H], op0=ALU.add, op1=ALU.mult
                                                   ).then_inc(kv_rows_ready, 1)

                def u_rows(b):
                    if not (isinstance(b, int) and b == 0):
                        dve.wait_ge(g_ready, TT * b)
                    nc.vector.scalar_tensor_tensor(out=u_gate, in0=ez[:, :, 2 * H:QVU], scalar=1.0,
                                                   in1=z[:, :, 2 * H:QVU], op0=ALU.add, op1=ALU.mult
                                                   ).then_inc(u_ready, 1)

                def add_product(b):
                    dve.wait_ge(xb_ready, b + 1)
                    for h in range(2):
                        dve.wait_ge(y_in_psum, 2 * b + h + 1)
                        rows = x[:, bass.ds(b * TT + 2 * h, 2), :].rearrange("p a n -> p (a n)")
                        i = nc.vector.tensor_tensor(rows, tr_ps[h][:, :], rows, ALU.add)
                    i.then_inc(x_mixed, 1)

                def mask_kv(b):
                    for k in range(KH):
                        dve.wait_ge(kv_in_psum, KH * b + k + 1)
                        nc.vector.tensor_tensor(kv[:, k, :], bank[2 + k][:, 0:P], head_mask[:, :], ALU.mult
                                                ).then_inc(kv_ready, 1)

                def out_stats(b):
                    dve.wait_ge(o_ready, 2 * (b + 1))
                    apart(dve)
                    for j in range(TT):
                        nc.vector.bn_stats(o_st[:, j, :], o[:, j, :]).then_inc(o_bn, 1)
                    dve.wait_ge(o_bn, TT * (b + 1))
                    apart(dve)
                    for j in range(TT):
                        nc.vector.bn_aggr(o_mean_var[:, j, :], o_st[:, j, :]).then_inc(o_stats, 1)

                def out_norm(b):
                    dve.wait_ge(o_rstd, b + 1)
                    for j in range(TT):
                        nc.vector.scalar_tensor_tensor(out=o[:, j, :], in0=o[:, j, :],
                                                       scalar=o_mean_var[:, j, 0:1], in1=g_row,
                                                       op0=ALU.subtract, op1=ALU.mult).then_inc(o_gained, 1)
                    for j in range(TT):
                        dve.wait_ge(o_gained, TT * b + j + 1)
                        nc.vector.scalar_tensor_tensor(out=o[:, j, :], in0=o[:, j, :],
                                                       scalar=o_rs[:, j:j + 1], in1=b_row,
                                                       op0=ALU.mult, op1=ALU.add).then_inc(o_normed, 1)

                def first():
                    dve.wait_ge(att_loaded, 6 * 16)
                    for j in range(TT):
                        add_bias(0, j)
                        if j:
                            kv_rows(0, j - 1)

                def step(i, prev, nxt, after):
                    kv_rows(i, TT - 1)
                    u_rows(i)
                    if after:
                        ln_stats(LN_ATT + i + 2, i + 2, x_ready, NCH + 1)
                    elif nxt:
                        ln_stats(2 * NCH, 0, x_mixed, 2)
                    if prev:
                        add_product(i - 1)
                    mask_kv(i)
                    if nxt:
                        dve.wait_ge(u_ready, i + 1)
                        add_bias_kv(i + 1, 0)
                        dve.wait_ge(xT_in_psum, KH * (LN_ATT + i + 2))
                        ln_apply(LN_ATT + i + 2, i + 2 if after else 0)
                        add_bias_u(i + 1, 0)
                    out_stats(i)
                    if not nxt:
                        router_top(NCH)
                    if nxt:
                        add_bias(i + 1, 1)
                    out_norm(i)
                    if nxt:
                        add_bias(i + 1, 2)
                        kv_rows(i + 1, 0)
                        kv_rows(i + 1, 1)
                        add_bias(i + 1, 3)
                        kv_rows(i + 1, 2)

                def last():
                    router_weights(NCH)
                    add_product(NCH - 1)
                    dve.wait_ge(xhi_ready, KH * (NCH + 1))
                    for k in range(KH):
                        nc.vector.tensor_tensor(xT_lo[:, 0, k, :], xT[:, k, :], xT_hi[:, 0, k, :],
                                                ALU.subtract).then_inc(xlo_ready, 1)

                attention_steps(dve, first, step, last)

            mixture(0)
            attention()
            mixture(1)

        @block.tensor
        def _(pe):
            pe.sem_inc(gu_ready, 2 * PRIME)
            pe.sem_inc(down_done, PRIME)

            def transpose_x(n):
                pe.wait_ge(xn_ready, n + 1)
                for k in range(KH):
                    for j in range(TT):
                        i = nc.tensor.transpose(tr_ps[k][:, j * P:(j + 1) * P],
                                                xn[:, j, k * P:(k + 1) * P], ident[:, :])
                    i.then_inc(xT_in_psum, 1)

            def route(n, m, ps=router_ps):
                pe.wait_ge(xT_ready, KH * (n + 1))
                if ps is router_ps:
                    pe.wait_ge(xlo_ready, KH * (m + 1))
                for j in range(TT):
                    for k in range(KH):
                        i = nc.tensor.matmul(ps[:, j * R:(j + 1) * R],
                                             xT[:, k, j * P:(j + 1) * P], rw[:, k, :],
                                             start=(k == 0), stop=(k == KH - 1))
                i.then_inc(router_in_psum, 1)

            def transpose_comb(m, ps=comb_ps):
                pe.wait_ge(comb_ready, 2 * (m + 1))
                for j in range(TT):
                    i = nc.tensor.transpose(ps[0:R, j * P:(j + 1) * P], comb[:, j, :], ident[:, :])
                i.then_inc(comb_in_psum, 1)

            def gate_up_shared(w, par):
                for k in range(KH):
                    for n, (a, b) in enumerate(PASSES):
                        mv = (xT_hi, xT_lo)[b]
                        i = nc.tensor.matmul(shared_ps[:, :], ws_gu[:, (a * KH + k) * P:(a * KH + k + 1) * P],
                                             mv[:, par, k, :], start=(k + n == 0),
                                             stop=(k == KH - 1 and n == len(PASSES) - 1))
                i.then_inc(gu_ready, 2)

            def gate_up_pair(w, u, i4, par):
                pe.wait_ge(prod_ready, w - 1)
                for t, ps in ((0, gate_ps[i4 % 2]), (1, up_ps[i4 % 2])):
                    for k in range(KH):
                        for n, (a, b) in enumerate(PASSES):
                            mv = (xT_hi, xT_lo)[b]
                            i = nc.tensor.matmul(
                                ps[:, :], wgu16[:, bass.ds((u - 1) * 2 * GU + a * GU + (k * 2 + t) * P, P)],
                                mv[:, par, k, :], start=(k + n == 0),
                                stop=(k == KH - 1 and n == len(PASSES) - 1))
                    i.then_inc(gu_ready, 1)

            def down_product(w, hi_, lo_, wts, first, last):
                pe.wait_ge(hi_ready, w + 1)
                pe.wait_ge(lo_ready, w + 1)
                for j in range(TT):
                    for n, (a, b) in enumerate(PASSES):
                        i = nc.tensor.matmul(y_ps[j // 2][:, (j % 2) * H:(j % 2 + 1) * H],
                                             (hi_, lo_)[b][:, j * P:(j + 1) * P], wts(a),
                                             start=(first and j % 2 == 0 and n == 0),
                                             stop=(last and j % 2 == 1 and n == len(PASSES) - 1),
                                             skip_group_check=True)
                i.then_inc(down_done, 1)

            def down_shared(w):
                down_product(w, act_hi_s[I:P, :], act_lo_s[I:P, :],
                             lambda a: ws_d[I:P, a * H:(a + 1) * H], True, False)

            def down_pair(w, u, i4, last=False):
                down_product(w, act_hi[i4], act_lo[i4],
                             lambda a: wd16[:, bass.ds((u - 1) * 2 * H + a * H, H)], False, last)

            def pairs_of(ph, c, q, par):
                for i in range(4):
                    u = 4 * q + 3 + i
                    gate_up_pair(unit(ph, c, u), u, 2 + i, par)
                    down_pair(unit(ph, c, u - 2), u - 2, i)

            def pairs(ph, c, q0, q1, par):
                with pe.Fori(q0, q1) as q:
                    pairs_of(ph, c, q, par)

            def chunk(ph, c, par, nxt):
                n, m = 2 * ph * NCH + c + 1, ph * NCH + c + 1
                gate_up_pair(unit(ph, c, 1), 1, 0, par)
                gate_up_pair(unit(ph, c, 2), 2, 1, par)
                pe.wait_ge(x_ready, ph * NCH + c + 1)
                down_shared(unit(ph, c, SHARED))
                pairs(ph, c, 0, 2, par)
                if nxt or ph == 0:
                    transpose_x(n)
                pairs(ph, c, 2, 4, par)
                if nxt:
                    route(n, m)
                pairs(ph, c, 4, 6, par)
                pairs_of(ph, c, 6, par)
                if nxt:
                    transpose_comb(m)
                gate_up_pair(unit(ph, c, PAIRS - 1), PAIRS - 1, 2, par)
                down_pair(unit(ph, c, PAIRS - 3), PAIRS - 3, 0)
                gate_up_pair(unit(ph, c, PAIRS), PAIRS, 3, par)
                down_pair(unit(ph, c, PAIRS - 2), PAIRS - 2, 1)
                if nxt:
                    gate_up_shared(unit(ph, c + 1, SHARED), 1 - par)
                down_pair(unit(ph, c, PAIRS - 1), PAIRS - 1, 2)
                down_pair(unit(ph, c, PAIRS), PAIRS, 3, last=True)

            def mixture(ph):
                if ph == 0:
                    transpose_x(0)
                    route(0, 0)
                    transpose_comb(0)
                    pe.wait_ge(w_lo, 2 + 2 + 2 * GROUPS)
                else:
                    pe.wait_ge(x_mixed, NCH + 1)
                    pe.wait_ge(combT_ready, NCH + 1)
                    pe.wait_ge(xlo_ready, KH * (NCH + 1))
                gate_up_shared(unit(ph, 0, SHARED), 0)
                with pe.Fori(0, NCH // 2 - 1) as cc:
                    chunk(ph, 2 * cc, 0, True)
                    chunk(ph, 2 * cc + 1, 1, True)
                chunk(ph, NCH - 2, 0, True)
                chunk(ph, NCH - 1, 1, False)

            def attention():
                def transpose_rows(dst, rows, done):
                    for k in range(KH):
                        for j in range(TT):
                            i = nc.tensor.transpose(dst[k][:, j * P:(j + 1) * P], rows(j, k), ident[:, :])
                        i.then_inc(done, 1)

                def transpose_batch(b):
                    pe.wait_ge(xn_ready, LN_ATT + b + 1)
                    if not (isinstance(b, int) and b < 2):
                        pe.wait_ge(o_ready, 2 * (b - 1))
                    transpose_rows(y_ps, lambda j, k: xn[:, j, k * P:(k + 1) * P], xT_in_psum)

                def project_kv(b, j):
                    if j == 0:
                        pe.wait_ge(xT_ready, KH * (LN_ATT + b + 1))
                    elif j >= 2:
                        pe.wait_ge(z_ready, 2 * (TT * b + j - 1))
                    for k in range(KH):
                        i = nc.tensor.matmul(bank[j % 2][:, :], xT[:, k, j * P:(j + 1) * P],
                                             w_att[:, k, 0:2 * H], start=(k == 0), stop=(k == KH - 1))
                    i.then_inc(proj_in_psum, 1)

                def project_u(b, j):
                    for k in range(KH):
                        i = nc.tensor.matmul(bank[2 + j % 2][:, 0:H], xT[:, k, j * P:(j + 1) * P],
                                             w_att[:, k, 2 * H:QVU], start=(k == 0), stop=(k == KH - 1))
                    i.then_inc(proj_in_psum, 1)

                def project(b, j):
                    project_kv(b, j)
                    project_u(b, j)

                def transpose_gated(b):
                    pe.wait_ge(g_ready, TT * (b + 1))
                    pe.wait_ge(x_mixed, b + 1)
                    transpose_rows(tr_ps, lambda j, k: o[:, j, k * P:(k + 1) * P], gT_in_psum)

                def out_product(b):
                    pe.wait_ge(gT_ready, KH * (b + 1))
                    for j in range(TT):
                        for k in range(KH):
                            i = nc.tensor.matmul(tr_ps[j // 2][:, (j % 2) * H:(j % 2 + 1) * H],
                                                 gT[:, k, j * P:(j + 1) * P], w_oa[:, k, :],
                                                 start=(k == 0), stop=(k == KH - 1))
                        if j % 2:
                            i.then_inc(y_in_psum, 1)

                def keys_values(b):
                    pe.wait_ge(kv_rows_ready, 2 * TT * (b + 1))
                    pe.wait_ge(xT_ready, KH * (LN_ATT + b + 2))
                    transpose_rows(y_ps, lambda j, k: z[:, j, k * P:(k + 1) * P], kT_in_psum)
                    for k in range(KH):
                        for j in range(TT):
                            i = nc.tensor.matmul(bank[2 + k][:, 0:P], z[:, j, k * P:(k + 1) * P],
                                                 z[:, j, H + k * P:H + (k + 1) * P],
                                                 start=(j == 0), stop=(j == TT - 1))
                        i.then_inc(kv_in_psum, 1)

                def query(b):
                    pe.wait_ge(qT_ready, KH * (b + 1))
                    pe.wait_ge(kv_ready, KH * (b + 1))
                    for j in range(TT):
                        for k in range(KH):
                            i = nc.tensor.matmul(y_ps[j // 2][:, (j % 2) * H + k * P:(j % 2) * H + (k + 1) * P],
                                                 qT[:, k, j * P:(j + 1) * P], kv[:, k, :],
                                                 start=True, stop=True)
                        if j % 2:
                            i.then_inc(o_in_psum, 1)

                def first():
                    pe.wait_ge(att_loaded, 6 * 16)
                    for j in range(TT):
                        project(0, j)

                def step(i, prev, nxt, after):
                    transpose_batch(i + 1)
                    if prev:
                        transpose_gated(i - 1)
                        out_product(i - 1)
                    keys_values(i)
                    if nxt:
                        project_kv(i + 1, 0)
                    query(i)
                    if nxt:
                        project_u(i + 1, 0)
                        for j in range(1, TT):
                            project(i + 1, j)

                def last():
                    route(2 * NCH, NCH, bank[0])
                    transpose_gated(NCH - 1)
                    transpose_comb(NCH, bank[1])
                    out_product(NCH - 1)

                attention_steps(pe, first, step, last)

            pe.wait_ge(consts, 3)
            pe.wait_ge(small_loaded, 48)
            mixture(0)
            attention()
            mixture(1)


_OUT_SHAPE = (8, 512, 256)


def kernel(**inputs):
    import numpy as np
    import concourse.bacc as bacc
    from concourse.bass_utils import run_bass_kernel_spmd as run

    a = {k: np.asarray(v) for k, v in inputs.items()}
    C, T, H = _OUT_SHAPE
    TT, KH = T // P, H // P
    E, I2, _ = a["L0_ffn_gate_up_proj"].shape
    I = I2 // 2

    def features_first(w):
        return w.reshape(w.shape[0], KH, P).transpose(2, 1, 0)

    laid = {
        "x": a["L0_attn_x"].reshape(C, P, TT, H),
        "gate_up": a["L0_ffn_gate_up_proj"].reshape(E // 2, 2, 2, I, KH, P).transpose(5, 0, 4, 2, 1, 3)
                   .reshape(P, E // 2, KH * 2 * P),
        "down": a["L0_ffn_down_proj"].reshape(E // 2, 2, H, I).transpose(1, 3, 0, 2).reshape(P, E // 2, H),
        "shared_gate_up": features_first(np.concatenate(
            [a["L0_ffn_shared_gate_w"], a["L0_ffn_shared_up_w"]])).reshape(P, KH * P),
        "shared_down": a["L0_ffn_shared_down_w"].T,
        "router": features_first(np.concatenate([a["L0_ffn_router_w"], a["L0_ffn_shared_expert_gate_w"]])),
        "w_qvu": np.concatenate([a["L0_attn_Wqk"], a["L0_attn_Wv"], a["L0_attn_Wu"]], axis=1)
                 .reshape(KH, P, 3 * H).transpose(1, 0, 2),
        "b_qvu": np.concatenate([a["L0_attn_bqk"], a["L0_attn_bv"], a["L0_attn_bu"]]),
        "w_o": a["L0_attn_Wo"].reshape(KH, P, H).transpose(1, 0, 2),
        "b_o": a["L0_attn_bo"],
        "ln_g": a["L0_attn_ln_g"],
        "ln_b": a["L0_attn_ln_b"],
    }
    nc = bacc.Bacc("TRN2", target_bir_lowering=False, num_devices=1)
    arrays, args = {}, []
    for name, v in laid.items():
        v = np.ascontiguousarray(v)
        arrays[f"in_{name}"] = v
        args.append(nc.dram_tensor(f"in_{name}", v.shape, mybir.dt.from_np(v.dtype), kind="ExternalInput").ap())
    args.append(nc.dram_tensor("result", (C, P, TT, H), F32, kind="ExternalOutput").ap())
    macaron_kernel(nc, *args)
    r = run(nc, [arrays], core_ids=[0])
    return r.results[0]["result"].reshape(_OUT_SHAPE)
```

```python
from contextlib import ExitStack

import concourse.bass as bass
from concourse import mybir

ALU = mybir.AluOpType
ACT = mybir.ActivationFunctionType
F32 = mybir.dt.float32
F16 = mybir.dt.float16
U32 = mybir.dt.uint32
AX_X = mybir.AxisListType.X
RMAX = bass.bass_isa.ReduceOp.max

P = 128


def macaron_kernel(nc, x_in, gate_up, down, shared_gate_up, shared_down, router,
                   w_qvu, b_qvu, w_o, b_o, ln_g, ln_b, out):
    NCH, _, TT, H = x_in.shape
    CH = P * TT
    KH = H // P
    PAIRS = gate_up.shape[1]
    E = 2 * PAIRS
    I = P // 2
    R = E + 1
    HD = 16
    QVU = 3 * H
    UNITS = PAIRS + 1
    TOPK = 8
    EPS = 1e-5
    LOWEST = -3.0e38

    GU = KH * 2 * P
    GROUP = 2
    SHIFT = 2 * GROUP
    GROUPS = PAIRS // GROUP
    LOADS = 8

    CW = 13
    COMB_SCALE = 2.0 ** (-4 - 2 * CW)

    ctx = ExitStack()
    with ctx:
        def sb(name, shape, dt):
            return ctx.enter_context(nc.sbuf_tensor(name, shape, dt))

        def sem(name):
            return ctx.enter_context(nc.semaphore(name))

        x = sb("x", [P, NCH * TT, H], F32)
        wgu = sb("wgu", [P, (PAIRS + SHIFT) * GU], F32)
        wd = sb("wd", [P, (PAIRS + SHIFT) * H], F32)
        wgu16 = wgu[:, :].bitcast(F16)
        wd16 = wd[:, :].bitcast(F16)
        ws_gu = sb("ws_gu", [P, 2 * KH * P], F16)
        ws_d = sb("ws_d", [P, 2 * H], F16)
        rw = sb("rw", [P, KH, R], F32)
        ident = sb("ident", [P, P], F32)
        head_mask = sb("head_mask", [P, P], F32)
        minus_half = sb("minus_half", [P, TT], F32)
        sc = sb("sc", [P, 8], F32)
        wmax = sb("wmax", [P, 2 * (LOADS + 1) + 4], F32)
        wmax_gu, wmax_d = wmax[:, 0:LOADS + 1], wmax[:, LOADS + 1:2 * (LOADS + 1)]
        wmax_row = wmax[:, 2 * (LOADS + 1):2 * (LOADS + 1) + 2]
        wmax_top = wmax[:, 2 * (LOADS + 1) + 2:2 * (LOADS + 1) + 4]
        stats = sb("stats", [P, TT, 6], F32)
        mean_var = sb("mean_var", [P, TT, 2], F32)
        var_eps = sb("var_eps", [P, TT], F32)
        rstd = sb("rstd", [P, TT], F32)
        o_st = sb("o_st", [P, TT, 6], F32)
        o_mean_var = sb("o_mean_var", [P, TT, 2], F32)
        o_var_eps = sb("o_var_eps", [P, TT], F32)
        o_rs = sb("o_rs", [P, TT], F32)
        xn = sb("xn", [P, TT, H], F32)
        xT = sb("xT", [P, KH, CH], F32)
        xT_hi = sb("xT_hi", [P, 2, KH, CH], F16)
        xT_lo = sb("xT_lo", [P, 2, KH, CH], F16)
        logits = sb("logits", [P, TT, R], F32)
        top = sb("top", [P, TT, TOPK], F32)
        replaced = sb("replaced", [P, TT, E], F32)
        expo = sb("expo", [P, TT, E], F32)
        shared_th = sb("shared_th", [P, TT], F32)
        top_sum = sb("top_sum", [P, TT], F32)
        top_rec = sb("top_rec", [P, TT], F32)
        comb = sb("comb", [P, TT, R], F32)
        combT = sb("combT", [P, 2, CH], F32)
        kv = sb("kv", [P, KH, P], F32)

        SCRATCH = 16 * CH
        scratch = sb("scratch", [P, SCRATCH], F32)
        at = [0]

        def part(n):
            at[0] += n
            assert at[0] <= SCRATCH
            return scratch[:, at[0] - n:at[0]]

        cb = [part(CH) for _ in range(4)]
        cb_s = part(CH)
        th = [part(CH) for _ in range(2)]
        th_s = part(CH)
        act = [part(CH) for _ in range(2)]
        act_s = part(CH)
        act_hi = [part(CH // 2).bitcast(F16) for _ in range(4)]
        act_lo = [part(CH // 2).bitcast(F16) for _ in range(4)]
        act_lo_hi_s = part(CH // 2).bitcast(F16)
        at[0] = 0
        z = part(TT * QVU).rearrange("p (j n) -> p j n", j=TT)
        ez = part(TT * QVU).rearrange("p (j n) -> p j n", j=TT)
        u_gate = part(TT * H).rearrange("p (j n) -> p j n", j=TT)
        o = part(TT * H).rearrange("p (j n) -> p j n", j=TT)
        qT = xT_hi[:, :, :, :].rearrange("p a k n -> p (a k n)").bitcast(F32).rearrange(
            "p (k n) -> p k n", k=KH)
        gT = xT_lo[:, :, :, :].rearrange("p a k n -> p (a k n)").bitcast(F32).rearrange(
            "p (k n) -> p k n", k=KH)
        gT_last = scratch[:, 8 * CH:8 * CH + KH * CH].rearrange("p (k n) -> p k n", k=KH)
        s_gu32 = scratch[:, 0:KH * P]
        s_d32 = scratch[:, KH * P:KH * P + H]
        w_att = wgu[:, PAIRS * GU:PAIRS * GU + KH * QVU].rearrange("p (k n) -> p k n", k=KH)
        w_oa = wgu[:, PAIRS * GU + KH * QVU:PAIRS * GU + KH * QVU + KH * H].rearrange(
            "p (k n) -> p k n", k=KH)
        assert SHIFT * GU >= KH * (QVU + H) and SHIFT * H >= H
        b_att = sb("b_att", [P, QVU], F32)
        g_row = wd[:, PAIRS * H:PAIRS * H + H]
        b_row = wd[:, PAIRS * H + H:PAIRS * H + 2 * H]
        bo_row = wd[:, PAIRS * H + 2 * H:PAIRS * H + 3 * H]

        combT_dram = nc.dram_tensor("combT_dram", (2, R, CH), F32, kind="Internal").ap()

        LN_ATT = NCH

        def attention_steps(engine, first, step, last):
            first()
            step(0, False, True, True)
            with engine.Fori(1, NCH - 2) as i:
                step(i, True, True, True)
            step(NCH - 2, True, True, False)
            step(NCH - 1, True, False, False)
            last()

        bank = [ctx.enter_context(nc.psum_tensor(f"bank{i}", [P, 512], F32)) for i in range(8)]
        gate_ps, up_ps, y_ps = bank[0:2], bank[2:4], bank[4:6]
        tr_ps = bank[6:8]
        shared_ps, router_ps, comb_ps = bank[6], bank[6], bank[7]

        early_shared_ps, early_router_ps, early_comb_ps = bank[4], bank[0], bank[1]

        x_loaded = sem("x_loaded")
        x_rest_loaded = sem("x_rest_loaded")
        w_loaded = [sem(f"w_loaded{i}") for i in range(LOADS)]
        small_loaded = sem("small_loaded")
        att_loaded = sem("att_loaded")
        waits_apart = sem("waits_apart")
        consts = sem("consts")
        const_step = sem("const_step")
        wmax_parts = sem("wmax_parts")
        wmax_rows = sem("wmax_rows")
        wmax_all = sem("wmax_all")
        scale_step = sem("scale_step")
        scales_ready = sem("scales_ready")
        w_hi = sem("w_hi")
        w_lo = sem("w_lo")
        bn_done = sem("bn_done")
        stats_ready = sem("stats_ready")
        var_ready = sem("var_ready")
        rstd_ready = sem("rstd_ready")
        xn_ready = sem("xn_ready")
        xT_in_psum = sem("xT_in_psum")
        xT_ready = sem("xT_ready")
        xhi_ready = sem("xhi_ready")
        xlo_ready = sem("xlo_ready")
        router_in_psum = sem("router_in_psum")
        logits_ready = sem("logits_ready")
        top_done = sem("top_done")
        replaced_done = sem("replaced_done")
        shifted_ready = sem("shifted_ready")
        exp_ready = sem("exp_ready")
        comb_step = sem("comb_step")
        comb_ready = sem("comb_ready")
        comb_in_psum = sem("comb_in_psum")
        combT_ready = sem("combT_ready")
        combT_stored = sem("combT_stored")
        cb_loaded = [sem(f"cb_loaded{i}") for i in range(4)]
        cbs_loaded = sem("cbs_loaded")
        gu_ready = sem("gu_ready")
        th_ready = sem("th_ready")
        gated = sem("gated")
        prod_ready = sem("prod_ready")
        act_ready = sem("act_ready")
        hi_ready = sem("hi_ready")
        lo_ready = sem("lo_ready")
        down_done = sem("down_done")
        x_ready = sem("x_ready")
        last_half_ready = sem("last_half_ready")
        out_stored = sem("out_stored")
        proj_in_psum = sem("proj_in_psum")
        z_ready = sem("z_ready")
        ez_ready = sem("ez_ready")
        em_ready = sem("em_ready")
        kv_rows_ready = sem("kv_rows_ready")
        u_ready = sem("u_ready")
        kv_in_psum = sem("kv_in_psum")
        kv_ready = sem("kv_ready")
        kT_in_psum = sem("kT_in_psum")
        qT_ready = sem("qT_ready")
        o_in_psum = sem("o_in_psum")
        o_ready = sem("o_ready")
        o_bn = sem("o_bn")
        o_stats = sem("o_stats")
        o_var = sem("o_var")
        o_rstd = sem("o_rstd")
        o_gained = sem("o_gained")
        o_normed = sem("o_normed")
        g_ready = sem("g_ready")
        gT_in_psum = sem("gT_in_psum")
        gT_ready = sem("gT_ready")
        xb_ready = sem("xb_ready")
        y_in_psum = sem("y_in_psum")
        x_mixed = sem("x_mixed")

        PRIME = 4

        def unit(ph, c, u):
            return PRIME + ph * NCH * UNITS + c * UNITS + u

        SHARED = 0

        PASSES = ((0, 0), (0, 1), (1, 0))

        def tiles(c):
            return x[:, bass.ds(c * TT, TT), :]

        def tile_of(c, j):
            return x[:, bass.ds(c * TT + j, 1), :].rearrange("p a n -> p (a n)")


        def gu32(g):
            return wgu[:, bass.ds((g * GROUP + SHIFT) * GU, GROUP * GU)].rearrange(
                "p (a n) -> p a n", a=GROUP)

        def d32(g):
            return wd[:, bass.ds((g * GROUP + SHIFT) * H, GROUP * H)].rearrange(
                "p (a n) -> p a n", a=GROUP)

        def gu_half(g, part_):
            return wgu16[:, bass.ds(g * GROUP * 2 * GU, GROUP * 2 * GU)].rearrange(
                "p (a s n) -> p a s n", a=GROUP, s=2)[:, :, part_, :]

        def d_half(g, part_):
            return wd16[:, bass.ds(g * GROUP * 2 * H, GROUP * 2 * H)].rearrange(
                "p (a s n) -> p a s n", a=GROUP, s=2)[:, :, part_, :]

        def converted(t):
            return t + 5

        def converts(ph, c):
            return ph == 0 and isinstance(c, int) and c == 0

        def follows_attention(ph, c):
            return ph == 1 and isinstance(c, int) and c == 0

        def convert_in_loop(q, i, convert_gu, convert_d):
            if i % 2 == 0:
                convert_d(2 * q + 2 + i // 2)
            elif not (isinstance(q, int) and 2 * q + 3 + i // 2 == GROUPS):
                convert_gu(2 * q + 3 + i // 2)

        def apart(engine):
            engine.sem_inc(waits_apart, 1)

        block = ctx.enter_context(nc.Block())

        @block.sync
        def _(sp):
            def load_x(c0, c1, done):
                sp.dma_start(x[:, c0 * TT:c1 * TT, :].rearrange("p (c j) h -> p c (j h)", c=c1 - c0),
                             x_in[c0:c1, :, :, :].rearrange("c p j h -> p c (j h)")).then_inc(done, 16)

            load_x(0, 2, x_loaded)
            sp.dma_start(rw[:, :, :], router).then_inc(small_loaded, 16)
            sp.dma_start(s_gu32, shared_gate_up).then_inc(small_loaded, 16)
            for rows in (slice(0, I), slice(I, P)):
                sp.dma_start(s_d32[rows, :], shared_down).then_inc(small_loaded, 16)
            n = PAIRS // LOADS
            for i in range(LOADS):
                sp.dma_start(wgu[:, (SHIFT + i * n) * GU:(SHIFT + (i + 1) * n) * GU],
                             gate_up[:, i * n:(i + 1) * n, :].rearrange("p a n -> p (a n)")
                             ).then_inc(w_loaded[i], 16)
                sp.dma_start(wd[:, (SHIFT + i * n) * H:(SHIFT + (i + 1) * n) * H],
                             down[:, i * n:(i + 1) * n, :].rearrange("p a n -> p (a n)")
                             ).then_inc(w_loaded[i], 16)
            load_x(2, NCH, x_rest_loaded)

            def spread(dst, par, row, done):
                src = combT_dram[par, bass.ds(row, 1), :].rearrange("a n -> (a n)")
                sp.dma_start(dst, src.partition_broadcast(I)).then_inc(done, 16)

            def pair(ph, c, u, par, i):
                sp.wait_ge(act_ready, unit(ph, c, u) - 3)
                src = combT_dram[par, bass.ds(2 * (u - 1), 2), :]
                sp.dma_start(cb[i][:, :], src[:, None, :].broadcast_to([2, I, CH])).then_inc(cb_loaded[i], 16)

            def chunk(ph, c, par, store_last=False):
                sp.wait_ge(combT_ready, ph * NCH + c + 1)
                sp.dma_start(combT_dram[par, :, :], combT[0:R, par, :]).then_inc(combT_stored, 16)
                sp.wait_ge(combT_stored, 16 * (ph * NCH + c + 1))
                if converts(ph, c):
                    sp.wait_ge(w_lo, 4)
                if follows_attention(ph, c):
                    sp.wait_ge(kv_in_psum, KH * NCH)
                    sp.wait_ge(u_ready, NCH)
                spread(cb_s[I:P, :], par, E, cbs_loaded)
                for i in range(4):
                    pair(ph, c, i + 1, par, i)
                if store_last:
                    store(c - 1)
                with sp.Fori(1, PAIRS // 4) as q:
                    for i in range(4):
                        pair(ph, c, 4 * q + i + 1, par, i)

            def store(c):
                sp.wait_ge(x_ready, NCH + c + 2)
                sp.dma_start(out[bass.ds(c, 1), :, :, :].rearrange("a p j h -> p (a j h)"),
                             tiles(c).rearrange("p j h -> p (j h)")).then_inc(out_stored, 16)

            chunk(0, 0, 0)
            sp.wait_ge(w_lo, converted(2 * GROUPS - 1))
            sp.dma_start(w_att, w_qvu).then_inc(att_loaded, 16)
            sp.dma_start(w_oa, w_o).then_inc(att_loaded, 16)
            sp.dma_start(b_att[:, :], b_qvu.partition_broadcast(P)).then_inc(att_loaded, 16)
            for row, vec in ((g_row, ln_g), (b_row, ln_b), (bo_row, b_o)):
                sp.dma_start(row, vec.partition_broadcast(P)).then_inc(att_loaded, 16)
            with sp.Fori(0, NCH // 2 - 1) as cc:
                chunk(0, 2 * cc + 1, 1)
                chunk(0, 2 * cc + 2, 0)
            chunk(0, NCH - 1, 1)
            chunk(1, 0, 0)
            with sp.Fori(0, NCH // 2 - 1) as cc:
                chunk(1, 2 * cc + 1, 1, True)
                chunk(1, 2 * cc + 2, 0, True)
            chunk(1, NCH - 1, 1, True)
            for h in range(2):
                sp.wait_ge(last_half_ready, h + 1)
                at_tile = (NCH - 1) * TT + 2 * h
                sp.dma_start(out[NCH - 1, :, 2 * h:2 * h + 2, :], x[:, at_tile:at_tile + 2, :]
                             ).then_inc(out_stored, 16)
            sp.wait_ge(out_stored, 16 * (NCH + 1))

        @block.gpsimd
        def _(pool):
            nc.gpsimd.memset(ident[:, :], 0.0).then_inc(const_step, 1)
            nc.gpsimd.memset(head_mask[:, :], 0.5).then_inc(const_step, 1)
            nc.gpsimd.memset(minus_half[:, :], -0.5).then_inc(consts, 1)
            pool.wait_ge(const_step, 2)
            nc.gpsimd.affine_select(out=ident[:, :], in_=ident[:, :], compare_op=ALU.not_equal, fill=1.0,
                                    base=0, pattern=[[-1, P]], channel_multiplier=1).then_inc(consts, 1)
            heads = head_mask[:, :].rearrange("p (a d) -> p a d", d=HD)
            nc.gpsimd.affine_select(out=heads, in_=heads, compare_op=ALU.is_ge, fill=0.0, base=0,
                                    pattern=[[-HD, P // HD], [0, HD]], channel_multiplier=1
                                    ).then_inc(const_step, 1)
            pool.wait_ge(const_step, 3)
            nc.gpsimd.affine_select(out=heads, in_=heads, compare_op=ALU.is_ge, fill=0.0, base=HD - 1,
                                    pattern=[[HD, P // HD], [0, HD]], channel_multiplier=-1
                                    ).then_inc(consts, 1)
            pool.sem_inc(act_ready, PRIME)

            def ln_rstd(n):
                pool.wait_ge(stats_ready, TT * (n + 1))
                apart(pool)
                nc.gpsimd.tensor_scalar(var_eps[:, :], mean_var[:, :, 1], EPS, None, ALU.add
                                        ).then_inc(var_ready, 1)
                pool.wait_ge(var_ready, n + 1)
                nc.gpsimd.tensor_tensor(rstd[:, :], var_eps[:, :], minus_half[:, :], ALU.pow
                                        ).then_inc(rstd_ready, 1)

            def weigh(w, buf, weights):
                pool.wait_ge(prod_ready, w + 1)
                nc.gpsimd.tensor_tensor(buf, buf, weights, ALU.mult).then_inc(act_ready, 1)

            def pair(ph, c, u, q, i):
                pool.wait_ge(cb_loaded[i], 16 * ((ph * NCH + c) * (PAIRS // 4) + q + 1))
                weigh(unit(ph, c, u), act[i % 2], cb[i])

            def pairs_of(ph, c, q):
                for i in range(4):
                    pair(ph, c, 4 * q + 3 + i, q + (2 + i) // 4, (2 + i) % 4)

            def pairs(ph, c, q0, q1):
                with pool.Fori(q0, q1) as q:
                    pairs_of(ph, c, q)

            def chunk(ph, c, par, nxt):
                pool.wait_ge(cbs_loaded, 16 * (ph * NCH + c + 1))
                pool.wait_ge(act_ready, unit(ph, c, SHARED))
                weigh(unit(ph, c, SHARED), act_s[I:P, :], cb_s[I:P, :])
                pool.wait_ge(act_ready, unit(ph, c, SHARED) + 1)
                pair(ph, c, 1, 0, 0)
                if nxt or ph == 0:
                    ln_rstd(2 * ph * NCH + c + 1)
                pair(ph, c, 2, 0, 1)
                pairs(ph, c, 0, 2)
                pairs(ph, c, 2, 4)
                if not nxt and ph == 0:
                    ln_rstd(LN_ATT + 1)
                pairs(ph, c, 4, 6)
                pairs_of(ph, c, 6)
                pair(ph, c, PAIRS - 1, PAIRS // 4 - 1, 2)
                pair(ph, c, PAIRS, PAIRS // 4 - 1, 3)

            def mixture(ph):
                if ph == 0:
                    ln_rstd(0)
                    pool.wait_ge(wmax_rows, 2)
                    nc.gpsimd.partition_all_reduce(wmax_top, wmax_row, P, RMAX).then_inc(wmax_all, 1)
                chunk(ph, 0, 0, True)
                with pool.Fori(0, NCH // 2 - 1) as cc:
                    chunk(ph, 2 * cc + 1, 1, True)
                    chunk(ph, 2 * cc + 2, 0, True)
                chunk(ph, NCH - 1, 1, False)

            def attention():
                def elu_low(b, j):
                    pool.wait_ge(ez_ready, 2 * (TT * b + j) + 1)
                    apart(pool)
                    nc.gpsimd.tensor_scalar(ez[:, j, 0:H], ez[:, j, 0:H], 1.0, -1.0, ALU.min, ALU.add
                                            ).then_inc(em_ready, 1)

                def out_rstd(b):
                    pool.wait_ge(o_stats, TT * (b + 1))
                    apart(pool)
                    nc.gpsimd.tensor_scalar(o_var_eps[:, :], o_mean_var[:, :, 1], EPS, None, ALU.add
                                            ).then_inc(o_var, 1)
                    pool.wait_ge(o_var, b + 1)
                    nc.gpsimd.tensor_tensor(o_rs[:, :], o_var_eps[:, :], minus_half[:, :], ALU.pow
                                            ).then_inc(o_rstd, 1)

                def add_bo(b):
                    pool.wait_ge(xn_ready, LN_ATT + b + 1)
                    nc.gpsimd.tensor_tensor(tiles(b), tiles(b),
                                            bo_row[:, None, :].broadcast_to([P, TT, H]), ALU.add
                                            ).then_inc(xb_ready, 1)

                def out_gate(b):
                    for j in range(TT - 1):
                        pool.wait_ge(o_normed, TT * b + j + 1)
                        nc.gpsimd.tensor_tensor(o[:, j, :], o[:, j, :], u_gate[:, j, :], ALU.mult
                                                ).then_inc(g_ready, 1)

                def first():
                    pool.wait_ge(att_loaded, 6 * 16)
                    for j in range(TT - 1):
                        elu_low(0, j)

                def step(i, prev, nxt, after):
                    elu_low(i, TT - 1)
                    if prev:
                        add_bo(i - 1)
                    if nxt:
                        ln_rstd(LN_ATT + i + 2)
                    if nxt:
                        elu_low(i + 1, 0)
                    out_rstd(i)
                    if nxt:
                        elu_low(i + 1, 1)
                    out_gate(i)
                    if nxt:
                        elu_low(i + 1, 2)

                def last():
                    add_bo(NCH - 1)
                    pool.wait_ge(xb_ready, NCH)

                attention_steps(pool, first, step, last)

            mixture(0)
            attention()
            mixture(1)

        @block.scalar
        def _(act_e):
            act_e.sem_inc(th_ready, PRIME)
            act_e.sem_inc(hi_ready, PRIME)
            act_e.sem_inc(w_hi, 2)

            def split_hi(out, in_, scale):
                nc.scalar.activation(out, in_, ACT.Copy, scale=scale).then_inc(w_hi, 1)

            def convert_gu(g):
                act_e.wait_ge(w_lo, 2 * g + 2)
                split_hi(gu_half(g, 0), gu32(g), sc[:, 2:3])

            def convert_d(g):
                act_e.wait_ge(w_lo, 2 * g + 3)
                split_hi(d_half(g, 0), d32(g), sc[:, 3:4])

            def xT_out(n, m, par, hi_too=True):
                act_e.wait_ge(xT_in_psum, KH * (n + 1))
                if not (isinstance(m, int) and m == 0):
                    act_e.wait_ge(router_in_psum, m)
                for k in range(KH):
                    nc.scalar.activation(xT[:, k, :], tr_ps[k][:, :], ACT.Copy).then_inc(xT_ready, 1)
                if hi_too:
                    for k in range(KH):
                        nc.scalar.activation(xT_hi[:, par, k, :], tr_ps[k][:, :], ACT.Copy
                                             ).then_inc(xhi_ready, 1)

            def logits_out(m, ps=router_ps):
                act_e.wait_ge(router_in_psum, m + 1)
                nc.scalar.activation(logits[:, :, :].rearrange("p j n -> p (j n)"),
                                     ps[:, 0:TT * R], ACT.Copy).then_inc(logits_ready, 1)

            def router_exp(m):
                act_e.wait_ge(shifted_ready, m + 1)
                nc.scalar.activation(expo[:, :, :], expo[:, :, :], ACT.Exp).then_inc(exp_ready, 1)
                nc.scalar.activation(shared_th[:, :], logits[:, :, E], ACT.Tanh, scale=0.5
                                     ).then_inc(exp_ready, 1)

            def comb_out(m, par, ps=comb_ps):
                act_e.wait_ge(comb_in_psum, m + 1)
                nc.scalar.activation(combT[0:R, par, :], ps[0:R, :], ACT.Copy, scale=COMB_SCALE
                                     ).then_inc(combT_ready, 1)

            def tanh(w, out, ps):
                act_e.wait_ge(gu_ready, 2 * w + 1)
                act_e.wait_ge(gated, w - 1)
                nc.scalar.activation(out, ps, ACT.Tanh, scale=sc[0:out.shape[0], 4:5]).then_inc(th_ready, 1)

            def hi(w, out, buf):
                act_e.wait_ge(act_ready, w + 1)
                act_e.wait_ge(down_done, w - 3)
                nc.scalar.activation(out, buf, ACT.Copy).then_inc(hi_ready, 1)

            def pair(ph, c, u, i, before):
                tanh(unit(ph, c, u), th[i % 2], gate_ps[i % 2][:, :])
                hi(unit(ph, c, u) - 1, act_hi[before], act[before % 2])

            def pairs_of(ph, c, q, first):
                for i in range(4):
                    if first:
                        convert_in_loop(q, i, convert_gu, convert_d)
                    pair(ph, c, 4 * q + 3 + i, (2 + i) % 4, (1 + i) % 4)

            def pairs(ph, c, q0, q1, first):
                with act_e.Fori(q0, q1) as q:
                    pairs_of(ph, c, q, first)

            def chunk(ph, c, par, nxt):
                n, m = 2 * ph * NCH + c + 1, ph * NCH + c + 1
                first = converts(ph, c)
                if not follows_attention(ph, c):
                    tanh(unit(ph, c, SHARED), th_s[0:I, :], shared_ps[0:I, :])
                if first:
                    convert_gu(1)
                hi(unit(ph, c, SHARED), act_lo_hi_s[I:P, :], act_s[I:P, :])
                tanh(unit(ph, c, 1), th[0], gate_ps[0][:, :])
                if first:
                    convert_d(1)
                pair(ph, c, 2, 1, 0)
                if first:
                    convert_gu(2)
                pairs(ph, c, 0, 2, first)
                if nxt or ph == 0:
                    xT_out(n, m, 1 - par, nxt)
                pairs(ph, c, 2, 4, first)
                if nxt:
                    logits_out(m)
                pairs(ph, c, 4, 6, first)
                if nxt:
                    router_exp(m)
                pairs_of(ph, c, 6, first)
                if nxt:
                    comb_out(m, 1 - par)
                pair(ph, c, PAIRS - 1, 2, 1)
                pair(ph, c, PAIRS, 3, 2)
                hi(unit(ph, c, PAIRS), act_hi[3], act[1])

            def mixture(ph):
                if ph == 0:
                    xT_out(0, 0, 0)
                    logits_out(0)
                    router_exp(0)
                    comb_out(0, 0)
                    act_e.wait_ge(scales_ready, 1)
                    split_hi(ws_gu[:, 0:KH * P], s_gu32, sc[:, 2:3])
                    split_hi(ws_d[:, 0:H], s_d32, sc[:, 3:4])
                    convert_gu(0)
                    convert_d(0)
                chunk(ph, 0, 0, True)
                with act_e.Fori(0, NCH // 2 - 1) as cc:
                    chunk(ph, 2 * cc + 1, 1, True)
                    chunk(ph, 2 * cc + 2, 0, True)
                chunk(ph, NCH - 1, 1, False)

            def attention():
                def copy_out(ready, b, src, dst, done, scale=1.0):
                    for k in range(KH):
                        act_e.wait_ge(ready, KH * b + k + 1)
                        nc.scalar.activation(dst(k), src[k][:, :], ACT.Copy, scale=scale).then_inc(done, 1)

                def exp_tanh(b, j):
                    act_e.wait_ge(z_ready, 2 * (TT * b + j) + 1)
                    nc.scalar.activation(ez[:, j, 0:H], z[:, j, 0:H], ACT.Exp).then_inc(ez_ready, 1)
                    act_e.wait_ge(z_ready, 2 * (TT * b + j) + 2)
                    nc.scalar.activation(ez[:, j, H:QVU], z[:, j, H:QVU], ACT.Tanh, scale=0.5
                                         ).then_inc(ez_ready, 1)

                def xT_copy(b):
                    copy_out(xT_in_psum, LN_ATT + b, y_ps, lambda k: xT[:, k, :], xT_ready)

                def gT_copy(b):
                    dst = gT_last if isinstance(b, int) and b == NCH - 1 else gT
                    copy_out(gT_in_psum, b, tr_ps, lambda k: dst[:, k, :], gT_ready, scale=0.5)

                def first():
                    for j in range(TT - 1):
                        exp_tanh(0, j)

                def step(i, prev, nxt, after):
                    if prev:
                        gT_copy(i - 1)
                    xT_copy(i + 1)
                    exp_tanh(i, TT - 1)
                    if not nxt:
                        logits_out(NCH, early_router_ps)
                    copy_out(kT_in_psum, i, y_ps, lambda k: qT[:, k, :], qT_ready)
                    if not nxt:
                        router_exp(NCH)
                    copy_out(o_in_psum, i, y_ps,
                             lambda h: o[:, 2 * h:2 * h + 2, :].rearrange("p j n -> p (j n)"), o_ready)
                    if nxt:
                        exp_tanh(i + 1, 0)
                        exp_tanh(i + 1, 1)
                        exp_tanh(i + 1, 2)

                def last():
                    for k in range(KH):
                        nc.scalar.activation(xT_hi[:, 0, k, :], xT[:, k, :], ACT.Copy
                                             ).then_inc(xhi_ready, 1)
                    comb_out(NCH, 0, early_comb_ps)
                    tanh(unit(1, 0, SHARED), th_s[0:I, :], early_shared_ps[0:I, :])
                    gT_copy(NCH - 1)

                attention_steps(act_e, first, step, last)

            mixture(0)
            attention()
            mixture(1)

        @block.vector
        def _(dve):
            for s in (gated, prod_ready, lo_ready):
                dve.sem_inc(s, PRIME)
            dve.sem_inc(x_ready, 1)
            dve.sem_inc(x_mixed, 1)
            dve.sem_inc(w_lo, 2)

            def split_lo(n, out, in_, scale, hi_in):
                dve.wait_ge(w_hi, n + 1)
                nc.vector.scalar_tensor_tensor(out=out, in0=in_, scalar=scale, in1=hi_in,
                                               op0=ALU.mult, op1=ALU.subtract).then_inc(w_lo, 1)

            def convert_gu(g):
                split_lo(2 * g + 4, gu_half(g, 1), gu32(g), sc[:, 2:3], gu_half(g, 0))

            def convert_d(g):
                split_lo(2 * g + 5, d_half(g, 1), d32(g), sc[:, 3:4], d_half(g, 0))

            def ln_stats(n, c, updated, count):
                dve.wait_ge(updated, count)
                for j in range(TT):
                    nc.vector.bn_stats(stats[:, j, :], tile_of(c, j)).then_inc(bn_done, 1)
                dve.wait_ge(bn_done, TT * (n + 1))
                apart(dve)
                for j in range(TT):
                    nc.vector.bn_aggr(mean_var[:, j, :], stats[:, j, :]).then_inc(stats_ready, 1)

            def ln_apply(n, c):
                dve.wait_ge(rstd_ready, n + 1)
                for j in range(TT):
                    i = nc.vector.tensor_scalar(xn[:, j, :], tile_of(c, j), mean_var[:, j, 0:1],
                                                rstd[:, j:j + 1], ALU.subtract, ALU.mult)
                i.then_inc(xn_ready, 1)

            def xT_low(m, par):
                dve.wait_ge(xhi_ready, KH * (m + 1))
                for k in range(KH):
                    nc.vector.tensor_tensor(xT_lo[:, par, k, :], tr_ps[k][:, :], xT_hi[:, par, k, :],
                                            ALU.subtract).then_inc(xlo_ready, 1)

            def router_top(m):
                dve.wait_ge(logits_ready, m + 1)
                apart(dve)
                for j in range(TT):
                    nc.vector.max(top[:, j, :], logits[:, j, 0:E]).then_inc(top_done, 1)
                dve.wait_ge(top_done, TT * (m + 1))
                apart(dve)
                for j in range(TT):
                    nc.vector.match_replace(replaced[:, j, :], top[:, j, :], logits[:, j, 0:E], LOWEST
                                            ).then_inc(replaced_done, 1)
                nc.vector.tensor_tensor(expo[:, :, :], logits[:, :, 0:E],
                                        top[:, :, 0:1].broadcast_to([P, TT, E]), ALU.subtract
                                        ).then_inc(shifted_ready, 1)
                dve.wait_ge(replaced_done, TT * (m + 1))
                nc.vector.tensor_tensor(replaced[:, :, :], logits[:, :, 0:E], replaced[:, :, :],
                                        ALU.not_equal).then_inc(comb_step, 1)

            def router_weights(m):
                dve.wait_ge(exp_ready, 2 * (m + 1))
                dve.wait_ge(comb_step, 4 * m + 1)
                nc.vector.tensor_tensor(expo[:, :, :], expo[:, :, :], replaced[:, :, :], ALU.mult
                                        ).then_inc(comb_step, 1)
                dve.wait_ge(comb_step, 4 * m + 2)
                nc.vector.reduce_sum(top_sum[:, :], expo[:, :, :], AX_X).then_inc(comb_step, 1)
                dve.wait_ge(comb_step, 4 * m + 3)
                nc.vector.reciprocal(top_rec[:, :], top_sum[:, :]).then_inc(comb_step, 1)
                nc.vector.tensor_scalar(comb[:, :, E], shared_th[:, :], 0.5, 0.5, ALU.mult, ALU.add
                                        ).then_inc(comb_ready, 1)
                dve.wait_ge(comb_step, 4 * m + 4)
                nc.vector.tensor_tensor(comb[:, :, 0:E], expo[:, :, :],
                                        top_rec[:, :, None].broadcast_to([P, TT, E]), ALU.mult
                                        ).then_inc(comb_ready, 1)

            def gate(w, buf, gate_in, up_in, th_in, buf_up=None):
                dve.wait_ge(lo_ready, w - 1)
                dve.wait_ge(th_ready, w + 1)
                nc.vector.scalar_tensor_tensor(out=buf, in0=th_in, scalar=1.0, in1=gate_in,
                                               op0=ALU.add, op1=ALU.mult).then_inc(gated, 1)
                dve.wait_ge(gu_ready, 2 * w + 2)
                dve.wait_ge(gated, w + 1)
                nc.vector.tensor_tensor(buf, buf, up_in, ALU.mult).then_inc(prod_ready, 1)

            def low(w, out, buf, hi_in):
                dve.wait_ge(hi_ready, w + 1)
                nc.vector.tensor_tensor(out, buf, hi_in, ALU.subtract).then_inc(lo_ready, 1)

            def low_s(w):
                low(w, act_lo_hi_s[0:I, :], act_s[I:P, :], act_lo_hi_s[I:P, :])

            def gate_s(w, ps=shared_ps):
                gate(w, act_s[I:P, :], ps[0:I, :], ps[I:P, :], th_s[0:I, :])

            def gate_pair(w, i):
                gate(w, act[i % 2], gate_ps[i % 2][:, :], up_ps[i % 2][:, :], th[i % 2])

            def pair(ph, c, u, i, before):
                gate_pair(unit(ph, c, u), i)
                low(unit(ph, c, u) - 1, act_lo[before], act[before % 2], act_hi[before])

            def pairs_of(ph, c, q, first):
                for i in range(4):
                    pair(ph, c, 4 * q + 3 + i, (2 + i) % 4, (1 + i) % 4)
                    if first:
                        convert_in_loop(q, i, convert_gu, convert_d)

            def pairs(ph, c, q0, q1, first):
                with dve.Fori(q0, q1) as q:
                    pairs_of(ph, c, q, first)

            def chunk(ph, c, par, nxt):
                n, m = 2 * ph * NCH + c + 1, ph * NCH + c + 1
                first = converts(ph, c)
                if first:
                    convert_gu(1)
                low_s(unit(ph, c, SHARED))
                gate_pair(unit(ph, c, 1), 0)
                if first:
                    convert_d(1)
                if ph == 0 and not nxt:
                    ln_stats(LN_ATT, 0, x_ready, 2)
                elif first:
                    ln_stats(n, c + 1, x_loaded, 16)
                elif ph == 0:
                    ln_stats(n, c + 1, x_rest_loaded, 16)
                elif nxt:
                    ln_stats(n, c + 1, x_mixed, NCH + 1)
                pair(ph, c, 2, 1, 0)
                if first:
                    convert_gu(2)
                if nxt:
                    ln_apply(n, c + 1)
                elif ph == 0:
                    ln_apply(LN_ATT, 0)
                pairs(ph, c, 0, 2, first)
                if nxt:
                    xT_low(m, 1 - par)
                elif ph == 0:
                    ln_stats(LN_ATT + 1, 1, x_ready, 3)
                pairs(ph, c, 2, 4, first)
                if nxt:
                    router_top(m)
                elif ph == 0:
                    dve.wait_ge(xT_in_psum, KH * (LN_ATT + 1))
                    ln_apply(LN_ATT + 1, 1)
                pairs(ph, c, 4, 6, first)
                if nxt:
                    router_weights(m)
                pairs_of(ph, c, 6, first)
                pair(ph, c, PAIRS - 1, 2, 1)
                pair(ph, c, PAIRS, 3, 2)
                low(unit(ph, c, PAIRS), act_lo[3], act[1], act_hi[3])
                if nxt:
                    gate_s(unit(ph, c + 1, SHARED))
                dve.wait_ge(down_done, unit(ph, c, PAIRS) + 1)
                for h in range(2):
                    rows = x[:, bass.ds(c * TT + 2 * h, 2), :].rearrange("p a n -> p (a n)")
                    i = nc.vector.scalar_tensor_tensor(out=rows, in0=y_ps[h][:, :], scalar=sc[:, 5:6],
                                                       in1=rows, op0=ALU.mult, op1=ALU.add)
                    if ph == 1 and not nxt:
                        i.then_inc(last_half_ready, 1)
                if ph == 0 or nxt:
                    i.then_inc(x_ready, 1)

            def ready_first():
                ln_stats(0, 0, x_loaded, 16)
                ln_apply(0, 0)
                shared_maxima()
                load_maxima(0)
                xT_low(0, 0)
                load_maxima(1)
                router_top(0)
                load_maxima(2)
                router_weights(0)
                for i in range(3, LOADS):
                    load_maxima(i)

            def shared_maxima():
                dve.wait_ge(small_loaded, 64)
                nc.vector.tensor_reduce(wmax_gu[:, LOADS:LOADS + 1], s_gu32, AX_X, ALU.max,
                                        apply_absolute_value=True).then_inc(wmax_parts, 1)
                nc.vector.tensor_reduce(wmax_d[:, LOADS:LOADS + 1], s_d32, AX_X, ALU.max,
                                        apply_absolute_value=True).then_inc(wmax_parts, 1)

            def load_maxima(i):
                n = PAIRS // LOADS
                dve.wait_ge(w_loaded[i], 32)
                nc.vector.tensor_reduce(wmax_gu[:, i:i + 1],
                                        wgu[:, (SHIFT + i * n) * GU:(SHIFT + (i + 1) * n) * GU],
                                        AX_X, ALU.max, apply_absolute_value=True).then_inc(wmax_parts, 1)
                nc.vector.tensor_reduce(wmax_d[:, i:i + 1],
                                        wd[:, (SHIFT + i * n) * H:(SHIFT + (i + 1) * n) * H],
                                        AX_X, ALU.max, apply_absolute_value=True).then_inc(wmax_parts, 1)

            def weight_scales():
                dve.wait_ge(wmax_parts, 2 * (LOADS + 1))
                nc.vector.tensor_reduce(wmax_row[:, 0:1], wmax_gu, AX_X, ALU.max).then_inc(wmax_rows, 1)
                nc.vector.tensor_reduce(wmax_row[:, 1:2], wmax_d, AX_X, ALU.max).then_inc(wmax_rows, 1)
                dve.wait_ge(wmax_all, 1)
                bits = sc[:, :].bitcast(U32)
                nc.vector.tensor_scalar(bits[:, 0:2], wmax_top.bitcast(U32), 0x7F800000, None,
                                        ALU.bitwise_and).then_inc(scale_step, 1)
                dve.wait_ge(scale_step, 1)
                nc.vector.tensor_scalar(sc[:, 0:2], sc[:, 0:2], 2.0 ** -63, None, ALU.max
                                        ).then_inc(scale_step, 1)
                dve.wait_ge(scale_step, 2)
                nc.vector.tensor_scalar(bits[:, 2:4], bits[:, 0:2], -1.0, float((254 + CW) << 23),
                                        ALU.mult, ALU.add).then_inc(scale_step, 1)
                nc.vector.tensor_scalar(sc[:, 4:5], sc[:, 0:1], 2.0 ** (-CW - 1), None, ALU.mult
                                        ).then_inc(scale_step, 1)
                nc.vector.tensor_scalar(sc[:, 6:7], sc[:, 0:1], sc[:, 0:1], 2.0 ** (2 - CW),
                                        ALU.mult, ALU.mult).then_inc(scale_step, 1)
                dve.wait_ge(scale_step, 5)
                nc.vector.tensor_scalar(sc[:, 5:6], sc[:, 6:7], sc[:, 1:2], None, ALU.mult
                                        ).then_inc(scale_step, 1)
                dve.wait_ge(scale_step, 6)
                dve.sem_inc(scales_ready, 1)
                split_lo(2, ws_gu[:, KH * P:2 * KH * P], s_gu32, sc[:, 2:3], ws_gu[:, 0:KH * P])
                split_lo(3, ws_d[:, H:2 * H], s_d32, sc[:, 3:4], ws_d[:, 0:H])
                convert_gu(0)
                convert_d(0)

            def mixture(ph):
                if ph == 0:
                    ready_first()
                    weight_scales()
                    gate_s(unit(0, 0, SHARED))
                chunk(ph, 0, 0, True)
                with dve.Fori(0, NCH // 2 - 1) as cc:
                    chunk(ph, 2 * cc + 1, 1, True)
                    chunk(ph, 2 * cc + 2, 0, True)
                chunk(ph, NCH - 1, 1, False)

            def attention():
                def add_bias_kv(b, j):
                    dve.wait_ge(proj_in_psum, 2 * (TT * b + j) + 1)
                    nc.vector.tensor_tensor(z[:, j, 0:2 * H], bank[j % 2][:, :], b_att[:, 0:2 * H],
                                            ALU.add).then_inc(z_ready, 1)

                def add_bias_u(b, j):
                    dve.wait_ge(proj_in_psum, 2 * (TT * b + j) + 2)
                    nc.vector.tensor_tensor(z[:, j, 2 * H:QVU], bank[2 + j % 2][:, 0:H],
                                            b_att[:, 2 * H:QVU], ALU.add).then_inc(z_ready, 1)

                def add_bias(b, j):
                    add_bias_kv(b, j)
                    add_bias_u(b, j)

                def kv_rows(b, j):
                    dve.wait_ge(em_ready, TT * b + j + 1)
                    nc.vector.scalar_tensor_tensor(out=z[:, j, 0:H], in0=z[:, j, 0:H], scalar=0.0,
                                                   in1=ez[:, j, 0:H], op0=ALU.max, op1=ALU.add
                                                   ).then_inc(kv_rows_ready, 1)
                    dve.wait_ge(ez_ready, 2 * (TT * b + j) + 2)
                    nc.vector.scalar_tensor_tensor(out=z[:, j, H:2 * H], in0=ez[:, j, H:2 * H], scalar=1.0,
                                                   in1=z[:, j, H:2 * H], op0=ALU.add, op1=ALU.mult
                                                   ).then_inc(kv_rows_ready, 1)

                def u_rows(b):
                    if not (isinstance(b, int) and b == 0):
                        dve.wait_ge(g_ready, TT * b)
                    nc.vector.scalar_tensor_tensor(out=u_gate, in0=ez[:, :, 2 * H:QVU], scalar=1.0,
                                                   in1=z[:, :, 2 * H:QVU], op0=ALU.add, op1=ALU.mult
                                                   ).then_inc(u_ready, 1)

                def add_product(b):
                    dve.wait_ge(xb_ready, b + 1)
                    for h in range(2):
                        dve.wait_ge(y_in_psum, 2 * b + h + 1)
                        rows = x[:, bass.ds(b * TT + 2 * h, 2), :].rearrange("p a n -> p (a n)")
                        i = nc.vector.tensor_tensor(rows, tr_ps[h][:, :], rows, ALU.add)
                    i.then_inc(x_mixed, 1)

                def mask_kv(b):
                    for k in range(KH):
                        dve.wait_ge(kv_in_psum, KH * b + k + 1)
                        nc.vector.tensor_tensor(kv[:, k, :], bank[2 + k][:, 0:P], head_mask[:, :], ALU.mult
                                                ).then_inc(kv_ready, 1)

                def out_stats(b):
                    for j in range(TT):
                        if j % 2 == 0:
                            dve.wait_ge(o_ready, 2 * b + j // 2 + 1)
                            apart(dve)
                        nc.vector.bn_stats(o_st[:, j, :], o[:, j, :]).then_inc(o_bn, 1)
                    dve.wait_ge(o_bn, TT * (b + 1))
                    apart(dve)
                    for j in range(TT):
                        nc.vector.bn_aggr(o_mean_var[:, j, :], o_st[:, j, :]).then_inc(o_stats, 1)

                def out_norm(b):
                    dve.wait_ge(o_rstd, b + 1)
                    for j in range(TT):
                        nc.vector.scalar_tensor_tensor(out=o[:, j, :], in0=o[:, j, :],
                                                       scalar=o_mean_var[:, j, 0:1], in1=g_row,
                                                       op0=ALU.subtract, op1=ALU.mult).then_inc(o_gained, 1)
                    for j in range(TT):
                        dve.wait_ge(o_gained, TT * b + j + 1)
                        nc.vector.scalar_tensor_tensor(out=o[:, j, :], in0=o[:, j, :],
                                                       scalar=o_rs[:, j:j + 1], in1=b_row,
                                                       op0=ALU.mult, op1=ALU.add).then_inc(o_normed, 1)
                    dve.wait_ge(o_normed, TT * (b + 1))
                    nc.vector.tensor_tensor(o[:, TT - 1, :], o[:, TT - 1, :], u_gate[:, TT - 1, :], ALU.mult
                                            ).then_inc(g_ready, 1)

                def first():
                    dve.wait_ge(att_loaded, 6 * 16)
                    for j in range(TT):
                        add_bias(0, j)
                        if j:
                            kv_rows(0, j - 1)

                def step(i, prev, nxt, after):
                    kv_rows(i, TT - 1)
                    u_rows(i)
                    if after:
                        ln_stats(LN_ATT + i + 2, i + 2, x_ready, NCH + 1)
                    elif nxt:
                        ln_stats(2 * NCH, 0, x_mixed, 2)
                    mask_kv(i)
                    if prev:
                        add_product(i - 1)
                    if nxt:
                        dve.wait_ge(u_ready, i + 1)
                        add_bias_kv(i + 1, 0)
                        dve.wait_ge(xT_in_psum, KH * (LN_ATT + i + 2))
                        ln_apply(LN_ATT + i + 2, i + 2 if after else 0)
                    else:
                        router_top(NCH)
                    out_stats(i)
                    if nxt:
                        add_bias_u(i + 1, 0)
                        add_bias(i + 1, 1)
                    else:
                        dve.wait_ge(xhi_ready, KH * (NCH + 1))
                        for k in range(KH):
                            nc.vector.tensor_tensor(xT_lo[:, 0, k, :], xT[:, k, :], xT_hi[:, 0, k, :],
                                                    ALU.subtract).then_inc(xlo_ready, 1)
                        router_weights(NCH)
                    out_norm(i)
                    if nxt:
                        add_bias(i + 1, 2)
                        kv_rows(i + 1, 0)
                        kv_rows(i + 1, 1)
                        add_bias(i + 1, 3)
                        kv_rows(i + 1, 2)

                def last():
                    gate_s(unit(1, 0, SHARED), early_shared_ps)
                    add_product(NCH - 1)

                attention_steps(dve, first, step, last)

            mixture(0)
            attention()
            mixture(1)

        @block.tensor
        def _(pe):
            pe.sem_inc(gu_ready, 2 * PRIME)
            pe.sem_inc(down_done, PRIME)

            def transpose_x(n):
                pe.wait_ge(xn_ready, n + 1)
                for k in range(KH):
                    for j in range(TT):
                        i = nc.tensor.transpose(tr_ps[k][:, j * P:(j + 1) * P],
                                                xn[:, j, k * P:(k + 1) * P], ident[:, :])
                    i.then_inc(xT_in_psum, 1)

            def route(n, m, ps=router_ps):
                pe.wait_ge(xT_ready, KH * (n + 1))
                if ps is router_ps:
                    pe.wait_ge(xlo_ready, KH * (m + 1))
                for j in range(TT):
                    for k in range(KH):
                        i = nc.tensor.matmul(ps[:, j * R:(j + 1) * R],
                                             xT[:, k, j * P:(j + 1) * P], rw[:, k, :],
                                             start=(k == 0), stop=(k == KH - 1))
                i.then_inc(router_in_psum, 1)

            def transpose_comb(m, ps=comb_ps):
                pe.wait_ge(comb_ready, 2 * (m + 1))
                for j in range(TT):
                    i = nc.tensor.transpose(ps[0:R, j * P:(j + 1) * P], comb[:, j, :], ident[:, :])
                i.then_inc(comb_in_psum, 1)

            def gate_up_shared(w, par, ps=shared_ps):
                for k in range(KH):
                    for n, (a, b) in enumerate(PASSES):
                        mv = (xT_hi, xT_lo)[b]
                        i = nc.tensor.matmul(ps[:, :], ws_gu[:, (a * KH + k) * P:(a * KH + k + 1) * P],
                                             mv[:, par, k, :], start=(k + n == 0),
                                             stop=(k == KH - 1 and n == len(PASSES) - 1))
                i.then_inc(gu_ready, 2)

            def gate_up_pair(w, u, i4, par):
                pe.wait_ge(prod_ready, w - 1)
                for t, ps in ((0, gate_ps[i4 % 2]), (1, up_ps[i4 % 2])):
                    for k in range(KH):
                        for n, (a, b) in enumerate(PASSES):
                            mv = (xT_hi, xT_lo)[b]
                            i = nc.tensor.matmul(
                                ps[:, :], wgu16[:, bass.ds((u - 1) * 2 * GU + a * GU + (k * 2 + t) * P, P)],
                                mv[:, par, k, :], start=(k + n == 0),
                                stop=(k == KH - 1 and n == len(PASSES) - 1))
                    i.then_inc(gu_ready, 1)

            def down_product(w, hi_, lo_, wts, last):
                pe.wait_ge(hi_ready, w + 1)
                pe.wait_ge(lo_ready, w + 1)
                for j in range(TT):
                    for n, (a, b) in enumerate(PASSES):
                        i = nc.tensor.matmul(y_ps[j // 2][:, (j % 2) * H:(j % 2 + 1) * H],
                                             (hi_, lo_)[b][:, j * P:(j + 1) * P], wts(a),
                                             start=False,
                                             stop=(last and j % 2 == 1 and n == len(PASSES) - 1),
                                             skip_group_check=True)
                i.then_inc(down_done, 1)

            def down_shared(w):
                pe.wait_ge(hi_ready, w + 1)
                pe.wait_ge(lo_ready, w + 1)
                for j in range(TT):
                    dst = y_ps[j // 2][:, (j % 2) * H:(j % 2 + 1) * H]
                    nc.tensor.matmul(dst, act_lo_hi_s[:, j * P:(j + 1) * P], ws_d[:, 0:H],
                                     start=(j % 2 == 0), stop=False, skip_group_check=True)
                    i = nc.tensor.matmul(dst, act_lo_hi_s[I:P, j * P:(j + 1) * P], ws_d[I:P, H:2 * H],
                                         start=False, stop=False, skip_group_check=True)
                i.then_inc(down_done, 1)

            def down_pair(w, u, i4, last=False):
                down_product(w, act_hi[i4], act_lo[i4],
                             lambda a: wd16[:, bass.ds((u - 1) * 2 * H + a * H, H)], last)

            def gate_up_first(ph, c, par):
                gate_up_pair(unit(ph, c, 1), 1, 0, par)
                gate_up_pair(unit(ph, c, 2), 2, 1, par)

            def pairs_of(ph, c, q, par, first):
                for i in range(4):
                    u = 4 * q + 3 + i
                    if first and i % 2 == 0:
                        pe.wait_ge(w_lo, converted(4 * q + 3 + i))
                    gate_up_pair(unit(ph, c, u), u, 2 + i, par)
                    down_pair(unit(ph, c, u - 2), u - 2, i)

            def pairs(ph, c, q0, q1, par, first):
                with pe.Fori(q0, q1) as q:
                    pairs_of(ph, c, q, par, first)

            def chunk(ph, c, par, nxt):
                n, m = 2 * ph * NCH + c + 1, ph * NCH + c + 1
                first = converts(ph, c)
                if first:
                    pe.wait_ge(w_lo, converted(1))
                if not follows_attention(ph, c):
                    gate_up_first(ph, c, par)
                pe.wait_ge(x_ready, ph * NCH + c + 1)
                down_shared(unit(ph, c, SHARED))
                pairs(ph, c, 0, 2, par, first)
                if nxt or ph == 0:
                    transpose_x(n)
                pairs(ph, c, 2, 4, par, first)
                if nxt:
                    route(n, m)
                pairs(ph, c, 4, 6, par, first)
                pairs_of(ph, c, 6, par, first)
                if nxt:
                    transpose_comb(m)
                if first:
                    pe.wait_ge(w_lo, converted(2 * GROUPS - 1))
                gate_up_pair(unit(ph, c, PAIRS - 1), PAIRS - 1, 2, par)
                down_pair(unit(ph, c, PAIRS - 3), PAIRS - 3, 0)
                gate_up_pair(unit(ph, c, PAIRS), PAIRS, 3, par)
                down_pair(unit(ph, c, PAIRS - 2), PAIRS - 2, 1)
                if nxt:
                    gate_up_shared(unit(ph, c + 1, SHARED), 1 - par)
                down_pair(unit(ph, c, PAIRS - 1), PAIRS - 1, 2)
                down_pair(unit(ph, c, PAIRS), PAIRS, 3, last=True)

            def mixture(ph):
                if ph == 0:
                    transpose_x(0)
                    route(0, 0)
                    transpose_comb(0)
                    pe.wait_ge(w_lo, 4)
                    gate_up_shared(unit(0, 0, SHARED), 0)
                else:
                    pe.wait_ge(x_mixed, NCH + 1)
                chunk(ph, 0, 0, True)
                with pe.Fori(0, NCH // 2 - 1) as cc:
                    chunk(ph, 2 * cc + 1, 1, True)
                    chunk(ph, 2 * cc + 2, 0, True)
                chunk(ph, NCH - 1, 1, False)

            def attention():
                def transpose_rows(dst, rows, done):
                    for k in range(KH):
                        for j in range(TT):
                            i = nc.tensor.transpose(dst[k][:, j * P:(j + 1) * P], rows(j, k), ident[:, :])
                        i.then_inc(done, 1)

                def transpose_batch(b):
                    pe.wait_ge(xn_ready, LN_ATT + b + 1)
                    if not (isinstance(b, int) and b < 2):
                        pe.wait_ge(o_ready, 2 * (b - 1))
                    transpose_rows(y_ps, lambda j, k: xn[:, j, k * P:(k + 1) * P], xT_in_psum)

                def project_kv(b, j):
                    if j == 0:
                        pe.wait_ge(xT_ready, KH * (LN_ATT + b + 1))
                    elif j >= 2:
                        pe.wait_ge(z_ready, 2 * (TT * b + j - 1))
                    for k in range(KH):
                        i = nc.tensor.matmul(bank[j % 2][:, :], xT[:, k, j * P:(j + 1) * P],
                                             w_att[:, k, 0:2 * H], start=(k == 0), stop=(k == KH - 1))
                    i.then_inc(proj_in_psum, 1)

                def project_u(b, j):
                    for k in range(KH):
                        i = nc.tensor.matmul(bank[2 + j % 2][:, 0:H], xT[:, k, j * P:(j + 1) * P],
                                             w_att[:, k, 2 * H:QVU], start=(k == 0), stop=(k == KH - 1))
                    i.then_inc(proj_in_psum, 1)

                def project(b, j):
                    project_kv(b, j)
                    project_u(b, j)

                def transpose_gated(b):
                    pe.wait_ge(g_ready, TT * (b + 1))
                    pe.wait_ge(x_mixed, b + 1)
                    transpose_rows(tr_ps, lambda j, k: o[:, j, k * P:(k + 1) * P], gT_in_psum)

                def out_product(b):
                    src = gT_last if isinstance(b, int) and b == NCH - 1 else gT
                    pe.wait_ge(gT_ready, KH * (b + 1))
                    for j in range(TT):
                        for k in range(KH):
                            i = nc.tensor.matmul(tr_ps[j // 2][:, (j % 2) * H:(j % 2 + 1) * H],
                                                 src[:, k, j * P:(j + 1) * P], w_oa[:, k, :],
                                                 start=(k == 0), stop=(k == KH - 1))
                        if j % 2:
                            i.then_inc(y_in_psum, 1)

                def keys_values(b):
                    pe.wait_ge(kv_rows_ready, 2 * TT * (b + 1))
                    pe.wait_ge(xT_ready, KH * (LN_ATT + b + 2))
                    transpose_rows(y_ps, lambda j, k: z[:, j, k * P:(k + 1) * P], kT_in_psum)
                    for k in range(KH):
                        for j in range(TT):
                            i = nc.tensor.matmul(bank[2 + k][:, 0:P], z[:, j, k * P:(k + 1) * P],
                                                 z[:, j, H + k * P:H + (k + 1) * P],
                                                 start=(j == 0), stop=(j == TT - 1))
                        i.then_inc(kv_in_psum, 1)

                def query(b):
                    pe.wait_ge(qT_ready, KH * (b + 1))
                    pe.wait_ge(kv_ready, KH * (b + 1))
                    for j in range(TT):
                        for k in range(KH):
                            i = nc.tensor.matmul(y_ps[j // 2][:, (j % 2) * H + k * P:(j % 2) * H + (k + 1) * P],
                                                 qT[:, k, j * P:(j + 1) * P], kv[:, k, :],
                                                 start=True, stop=True)
                        if j % 2:
                            i.then_inc(o_in_psum, 1)

                def first():
                    pe.wait_ge(att_loaded, 6 * 16)
                    for j in range(TT):
                        project(0, j)

                def step(i, prev, nxt, after):
                    if prev:
                        transpose_gated(i - 1)
                    transpose_batch(i + 1)
                    if prev:
                        out_product(i - 1)
                    if not nxt:
                        route(2 * NCH, NCH, early_router_ps)
                    keys_values(i)
                    if nxt:
                        project_kv(i + 1, 0)
                    query(i)
                    if nxt:
                        project_u(i + 1, 0)
                        for j in range(1, TT):
                            project(i + 1, j)

                def last():
                    pe.wait_ge(o_ready, 2 * NCH)
                    pe.wait_ge(xlo_ready, KH * (NCH + 1))
                    gate_up_shared(unit(1, 0, SHARED), 0, early_shared_ps)
                    transpose_comb(NCH, early_comb_ps)
                    pe.wait_ge(combT_ready, NCH + 1)
                    gate_up_first(1, 0, 0)
                    transpose_gated(NCH - 1)
                    out_product(NCH - 1)

                attention_steps(pe, first, step, last)

            pe.wait_ge(consts, 3)
            pe.wait_ge(small_loaded, 64)
            mixture(0)
            attention()
            mixture(1)


_OUT_SHAPE = (8, 512, 256)


def kernel(**inputs):
    import numpy as np
    import concourse.bacc as bacc
    from concourse.bass_utils import run_bass_kernel_spmd as run

    a = {k: np.asarray(v) for k, v in inputs.items()}
    C, T, H = _OUT_SHAPE
    TT, KH = T // P, H // P
    E, I2, _ = a["L0_ffn_gate_up_proj"].shape
    I = I2 // 2

    def features_first(w):
        return w.reshape(w.shape[0], KH, P).transpose(2, 1, 0)

    laid = {
        "x": a["L0_attn_x"].reshape(C, P, TT, H),
        "gate_up": a["L0_ffn_gate_up_proj"].reshape(E // 2, 2, 2, I, KH, P).transpose(5, 0, 4, 2, 1, 3)
                   .reshape(P, E // 2, KH * 2 * P),
        "down": a["L0_ffn_down_proj"].reshape(E // 2, 2, H, I).transpose(1, 3, 0, 2).reshape(P, E // 2, H),
        "shared_gate_up": features_first(np.concatenate(
            [a["L0_ffn_shared_gate_w"], a["L0_ffn_shared_up_w"]])).reshape(P, KH * P),
        "shared_down": a["L0_ffn_shared_down_w"].T,
        "router": features_first(np.concatenate([a["L0_ffn_router_w"], a["L0_ffn_shared_expert_gate_w"]])),
        "w_qvu": np.concatenate([a["L0_attn_Wqk"], a["L0_attn_Wv"], a["L0_attn_Wu"]], axis=1)
                 .reshape(KH, P, 3 * H).transpose(1, 0, 2),
        "b_qvu": np.concatenate([a["L0_attn_bqk"], a["L0_attn_bv"], a["L0_attn_bu"]]),
        "w_o": a["L0_attn_Wo"].reshape(KH, P, H).transpose(1, 0, 2),
        "b_o": a["L0_attn_bo"],
        "ln_g": a["L0_attn_ln_g"],
        "ln_b": a["L0_attn_ln_b"],
    }
    nc = bacc.Bacc("TRN2", target_bir_lowering=False, num_devices=1)
    arrays, args = {}, []
    for name, v in laid.items():
        v = np.ascontiguousarray(v)
        arrays[f"in_{name}"] = v
        args.append(nc.dram_tensor(f"in_{name}", v.shape, mybir.dt.from_np(v.dtype), kind="ExternalInput").ap())
    args.append(nc.dram_tensor("result", (C, P, TT, H), F32, kind="ExternalOutput").ap())
    macaron_kernel(nc, *args)
    r = run(nc, [arrays], core_ids=[0])
    return r.results[0]["result"].reshape(_OUT_SHAPE)
```
